# Optimizing a Trainium2 kernel written in Bass

```python
import numpy as np
import jax
import jax.numpy as jnp

def _softmax(x, axis=-1):
    return jax.nn.softmax(x, axis=axis)

def _gelu(x):
    return jax.nn.gelu(x, approximate=True)

def _silu(x):
    return jax.nn.silu(x)

def _sigmoid(x):
    return jax.nn.sigmoid(x)

def _layernorm(x, axis=-1, eps=1e-05):
    m = jnp.mean(x, axis=axis, keepdims=True)
    v = jnp.var(x, axis=axis, keepdims=True)
    return (x - m) / jnp.sqrt(v + eps)

def _scatter_add(tgt, idx, src, axis=0):
    return tgt.at[idx].add(src)

def _segment_sum(src, seg, n):
    return jax.ops.segment_sum(src, seg, n)
kernel_name = 'mk_xattn_ffn_d4_seqx_r8_6b9866'

def setup_inputs(seed: int=0):
    np.random.seed(seed)
    _w = jnp.asarray

    def _rec_inputs():
        import jax
        import jax.numpy as jnp
        _rk = jax.random.key(seed)
        x = -0.0002928 + 1 * jax.random.normal(jax.random.fold_in(_rk, 1), (32, 56, 128), jnp.float32)
        _lenS = 56 - jax.random.randint(jax.random.fold_in(_rk, 7), (32,), 0, max(1, 56 // 4) + 1, jnp.int32)
        _lenS2 = 1500 - jax.random.randint(jax.random.fold_in(_rk, 8), (32,), 0, max(1, 1500 // 4) + 1, jnp.int32)
        _ctx_512P = jax.random.normal(jax.random.fold_in(_rk, 11), (32, 16, 64), jnp.float32)
        _ctx_512c = jax.random.dirichlet(jax.random.fold_in(_rk, 511), 0.3 * jnp.ones((16,), jnp.float32), (32, 1500))
        _ctx_512t = jnp.einsum('bsk,bkd->bsd', _ctx_512c, _ctx_512P)
        _ctx_512t = _ctx_512t * jax.lax.rsqrt(jnp.mean(jnp.square(_ctx_512t)) + 1e-12) * 0.953939
        ctx_512 = -1.52775e-05 + 0.999936 * (_ctx_512t + 0.3 * jax.random.normal(jax.random.fold_in(_rk, 611), (32, 1500, 64), jnp.float32))
        return (x, ctx_512)
    x, ctx_512 = _rec_inputs()

    def _L0_xattn_setup():
        import jax, jax.numpy as jnp
        import numpy as np
        NUM_HEADS = 16
        HEAD_DIM = 64
        Q_DIM = 128
        KV_DIM = 64
        INNER = NUM_HEADS * HEAD_DIM
        key = jax.random.key(seed)
        ks = jax.random.split(key, 7)
        B, N, M = (32, 128, 256)
        q = jax.random.normal(ks[0], (B, N, Q_DIM), dtype=jnp.float32)
        kv = jax.random.normal(ks[1], (B, M, KV_DIM), dtype=jnp.float32)
        Wq = jax.random.normal(ks[2], (Q_DIM, INNER), dtype=jnp.float32) / np.sqrt(Q_DIM)
        Wk = jax.random.normal(ks[3], (KV_DIM, INNER), dtype=jnp.float32) / np.sqrt(KV_DIM)
        Wv = jax.random.normal(ks[4], (KV_DIM, INNER), dtype=jnp.float32) / np.sqrt(KV_DIM)
        Wo = jax.random.normal(ks[5], (INNER, Q_DIM), dtype=jnp.float32) / np.sqrt(INNER)
        bo = jax.random.normal(ks[6], (Q_DIM,), dtype=jnp.float32) * 0.01
        return {'q': q, 'kv': kv, 'Wq': Wq, 'Wk': Wk, 'Wv': Wv, 'Wo': Wo, 'bo': bo}
    _L0_xattn_all = _L0_xattn_setup()
    _L0_xattn_in = {k: v for k, v in _L0_xattn_all.items() if k in ('Wq', 'Wk', 'Wv', 'Wo', 'bo')}
    del _L0_xattn_all

    def _L0_ffn_setup():
        import jax, jax.numpy as jnp
        import numpy as np
        E, H, F, K = (8, 128, 256, 2)
        B, S = (2, 256)
        key = jax.random.key(seed)
        ks = jax.random.split(key, 8)

        def w(k, shape, fan_in):
            return jax.random.normal(k, shape, jnp.float32) / np.float32(np.sqrt(fan_in))
        return {'x': jax.random.normal(ks[0], (B, S, H), jnp.float32), 'Wgate': w(ks[1], (H, E), H), 'bgate': jnp.zeros((E,), jnp.float32), 'W1': w(ks[2], (E, H, F), H), 'b1': jnp.zeros((E, F), jnp.float32), 'W2': w(ks[3], (E, H, F), H), 'b2': jnp.zeros((E, F), jnp.float32), 'Wg': w(ks[4], (E, F, F), F), 'bg': jnp.zeros((E, F), jnp.float32), 'Wl': w(ks[5], (E, F, F), F), 'bl': jnp.zeros((E, F), jnp.float32), 'W3': w(ks[6], (E, F, H), F), 'b3': jnp.zeros((E, H), jnp.float32)}
    _L0_ffn_all = _L0_ffn_setup()
    _L0_ffn_in = {k: v for k, v in _L0_ffn_all.items() if k in ('Wgate', 'bgate', 'W1', 'b1', 'W2', 'b2', 'Wg', 'bg', 'Wl', 'bl', 'W3', 'b3')}
    del _L0_ffn_all

    def _L1_xattn_setup():
        import jax, jax.numpy as jnp
        import numpy as np
        DIM = 128
        LATENT_DIM = 64
        NUM_HEADS = 16
        HEAD_DIM = DIM // NUM_HEADS
        SCALE = HEAD_DIM ** (-0.5)
        key = jax.random.key(seed)
        k1, k2, k3, k4, k5 = jax.random.split(key, 5)
        B, xN, zN = (2, 256, 256)
        x = jax.random.normal(k1, (B, xN, DIM), dtype=jnp.float32)
        z = jax.random.normal(k2, (B, zN, LATENT_DIM), dtype=jnp.float32)
        Wq = jax.random.normal(k3, (DIM, DIM), dtype=jnp.float32) * DIM ** (-0.5)
        Wkv = jax.random.normal(k4, (2 * DIM, LATENT_DIM), dtype=jnp.float32) * LATENT_DIM ** (-0.5)
        Wo = jax.random.normal(k5, (DIM, DIM), dtype=jnp.float32) * DIM ** (-0.5)
        return {'x': x, 'z': z, 'Wq': Wq, 'Wkv': Wkv, 'Wo': Wo}
    _L1_xattn_all = _L1_xattn_setup()
    _L1_xattn_in = {k: v for k, v in _L1_xattn_all.items() if k in ('Wq', 'Wkv', 'Wo')}
    del _L1_xattn_all

    def _L1_ffn_setup():
        import jax, jax.numpy as jnp
        import numpy as np
        INT8_MAX = 127.0

        def _absmax_scale(x, axes):
            amax = jnp.max(jnp.abs(x), axis=axes, keepdims=True)
            return jnp.maximum(amax, 1e-12) / INT8_MAX
        key = jax.random.key(seed)
        k1, k2 = jax.random.split(key)
        lhs = jax.random.normal(k1, (4, 1024, 128), dtype=jnp.float32)
        rhs = jax.random.normal(k2, (128, 128), dtype=jnp.float32)
        return {'lhs': lhs, 'rhs': rhs}
    _L1_ffn_all = _L1_ffn_setup()
    _L1_ffn_in = {k: v for k, v in _L1_ffn_all.items() if k in ('rhs',)}
    del _L1_ffn_all

    def _L2_xattn_setup():
        import jax, jax.numpy as jnp
        import numpy as np
        HEADS = 16
        D_MODEL = 128
        IMG_MODEL = 64
        D_K = D_MODEL // HEADS
        key = jax.random.key(seed)
        ks = jax.random.split(key, 12)
        B, LQ, LKV = (8, 256, 128)
        s_dm = 1.0 / np.sqrt(D_MODEL)
        s_im = 1.0 / np.sqrt(IMG_MODEL)
        return {'q': jax.random.normal(ks[0], (B, LQ, D_MODEL), jnp.float32), 'k': jax.random.normal(ks[1], (B, LKV, IMG_MODEL), jnp.float32), 'v': jax.random.normal(ks[2], (B, LKV, IMG_MODEL), jnp.float32), 'Wq': jax.random.normal(ks[3], (D_MODEL, D_MODEL), jnp.float32) * s_dm, 'bq': jnp.zeros((D_MODEL,), jnp.float32), 'Wk': jax.random.normal(ks[4], (IMG_MODEL, D_MODEL), jnp.float32) * s_im, 'bk': jnp.zeros((D_MODEL,), jnp.float32), 'Wv': jax.random.normal(ks[5], (IMG_MODEL, D_MODEL), jnp.float32) * s_im, 'bv': jnp.zeros((D_MODEL,), jnp.float32), 'Wo': jax.random.normal(ks[6], (D_MODEL, D_MODEL), jnp.float32) * s_dm, 'bo': jnp.zeros((D_MODEL,), jnp.float32)}
    _L2_xattn_all = _L2_xattn_setup()
    _L2_xattn_in = {k: v for k, v in _L2_xattn_all.items() if k in ('Wq', 'bq', 'Wk', 'bk', 'Wv', 'bv', 'Wo', 'bo')}
    del _L2_xattn_all

    def _L2_ffn_setup():
        import jax, jax.numpy as jnp
        import numpy as np
        B, N, D = (4, 256, 128)
        SPARSITY = 0.01
        key = jax.random.key(seed)
        k1, k2, k3 = jax.random.split(key, 3)
        x = jax.random.normal(k1, (B, N, D), dtype=jnp.float32)
        spatial = jax.random.normal(k2, (D, D), dtype=jnp.float32) * 0.02
        freq = jnp.fft.fft(spatial, axis=-1)
        k = int(D * SPARSITY)
        mag = jnp.abs(freq)
        kth = jax.lax.top_k(mag, k)[0][:, -1:]
        w_sparse = jnp.where(mag >= kth, freq, 0.0 + 0j)
        bias = jax.random.normal(k3, (D,), dtype=jnp.float32) * 0.01
        return {'x': x, 'w_freq_real': jnp.real(w_sparse).astype(jnp.float32), 'w_freq_imag': jnp.imag(w_sparse).astype(jnp.float32), 'bias': bias}
    _L2_ffn_all = _L2_ffn_setup()
    _L2_ffn_in = {k: v for k, v in _L2_ffn_all.items() if k in ('w_freq_real', 'w_freq_imag', 'bias')}
    del _L2_ffn_all

    def _L3_xattn_setup():
        import jax, jax.numpy as jnp
        import numpy as np
        H, D, C1, C2, S, M, B, W = (16, 32, 128, 64, 256, 64, 2, 4)

        def _ln(x, g, b):
            m = jnp.mean(x, -1, keepdims=True)
            v = jnp.var(x, -1, keepdims=True)
            return (x - m) * jax.lax.rsqrt(v + 1e-05) * g + b

        def _mha(x, y, wq, wk, wv, li1_w, li1_b, lnx_g, lnx_b, lny_g, lny_b, ln3_g, ln3_b, li2_w, li2_b, li3_w, li3_b, causal):
            xn = _ln(x, lnx_g, lnx_b)
            yn = _ln(y, lny_g, lny_b)
            q = jnp.einsum('bsc,hcd->bhsd', xn, wq)
            k = jnp.einsum('btc,hcd->bhtd', yn, wk)
            v = jnp.einsum('btc,hcd->bhtd', yn, wv)
            a = jax.nn.softmax(jnp.einsum('bhsd,bhtd->bhst', q, k) * D ** (-0.5), axis=-1)
            if causal:
                s, t = (a.shape[-2], a.shape[-1])
                mask = (jnp.arange(t)[None, :] > jnp.arange(s)[:, None]).astype(a.dtype)
                a = a * mask
            o = jnp.einsum('bhst,bhtd->bhsd', a, v)
            o = o.transpose(0, 2, 1, 3).reshape(x.shape[0], x.shape[1], H * D)
            x_out = x + o @ li1_w + li1_b
            h = jax.nn.gelu(_ln(x_out, ln3_g, ln3_b) @ li2_w + li2_b, approximate=False)
            return x_out + h @ li3_w + li3_b
        key = jax.random.key(seed)
        ks = iter(jax.random.split(key, 64))

        def w(shape, scale=0.02):
            return jax.random.normal(next(ks), shape, jnp.float32) * scale
        inp = {'xx': jax.random.normal(next(ks), (B, S, C1), jnp.float32), 'ee': jax.random.normal(next(ks), (B, M, C2), jnp.float32), 'ln1_g': jnp.ones(C1, jnp.float32), 'ln1_b': jnp.zeros(C1, jnp.float32), 'ln2_g': jnp.ones(C1, jnp.float32), 'ln2_b': jnp.zeros(C1, jnp.float32)}
        for pfx, cy in (('a1', C1), ('a2', C2)):
            inp[pfx + '_wq'] = w((H, C1, D))
            inp[pfx + '_wk'] = w((H, cy, D))
            inp[pfx + '_wv'] = w((H, cy, D))
            inp[pfx + '_li1_w'] = w((H * D, C1))
            inp[pfx + '_li1_b'] = jnp.zeros(C1, jnp.float32)
            inp[pfx + '_lnx_g'] = jnp.ones(C1, jnp.float32)
            inp[pfx + '_lnx_b'] = jnp.zeros(C1, jnp.float32)
            inp[pfx + '_lny_g'] = jnp.ones(cy, jnp.float32)
            inp[pfx + '_lny_b'] = jnp.zeros(cy, jnp.float32)
            inp[pfx + '_ln3_g'] = jnp.ones(C1, jnp.float32)
            inp[pfx + '_ln3_b'] = jnp.zeros(C1, jnp.float32)
            inp[pfx + '_li2_w'] = w((C1, C1 * W))
            inp[pfx + '_li2_b'] = jnp.zeros(C1 * W, jnp.float32)
            inp[pfx + '_li3_w'] = w((C1 * W, C1))
            inp[pfx + '_li3_b'] = jnp.zeros(C1, jnp.float32)
        inp['training'] = 0
        return inp
    _L3_xattn_all = _L3_xattn_setup()
    _L3_xattn_in = {k: v for k, v in _L3_xattn_all.items() if k in ('ln1_g', 'ln1_b', 'ln2_g', 'ln2_b', 'a1_wq', 'a1_wk', 'a1_wv', 'a1_li1_w', 'a1_li1_b', 'a1_lnx_g', 'a1_lnx_b', 'a1_lny_g', 'a1_lny_b', 'a1_ln3_g', 'a1_ln3_b', 'a1_li2_w', 'a1_li2_b', 'a1_li3_w', 'a1_li3_b', 'a2_wq', 'a2_wk', 'a2_wv', 'a2_li1_w', 'a2_li1_b', 'a2_lnx_g', 'a2_lnx_b', 'a2_lny_g', 'a2_lny_b', 'a2_ln3_g', 'a2_ln3_b', 'a2_li2_w', 'a2_li2_b', 'a2_li3_w', 'a2_li3_b')}
    del _L3_xattn_all

    def _L3_ffn_setup():
        import jax, jax.numpy as jnp
        import numpy as np
        IN_F, OUT_F, BLOCK, NBLK = (128, 512, 32, 16)
        TOPK = NBLK // 4
        key = jax.random.key(seed)
        ks = jax.random.split(key, 7)
        s = 1.0 / np.sqrt(IN_F)
        s2 = 1.0 / np.sqrt(OUT_F)
        return {'x': jax.random.normal(ks[0], (4, 512, IN_F), jnp.float32), 'router_w': jax.random.uniform(ks[1], (NBLK, IN_F), jnp.float32, -s, s), 'router_b': jax.random.uniform(ks[2], (NBLK,), jnp.float32, -s, s), 'w1': jax.random.uniform(ks[3], (OUT_F, IN_F), jnp.float32, -s, s), 'b1': jax.random.uniform(ks[4], (OUT_F,), jnp.float32, -s, s), 'w2': jax.random.uniform(ks[5], (IN_F, OUT_F), jnp.float32, -s2, s2), 'b2': jax.random.uniform(ks[6], (IN_F,), jnp.float32, -s2, s2)}
    _L3_ffn_all = _L3_ffn_setup()
    _L3_ffn_in = {k: v for k, v in _L3_ffn_all.items() if k in ('router_w', 'router_b', 'w1', 'b1', 'w2', 'b2')}
    del _L3_ffn_all
    return {'x': x, 'ctx_512': ctx_512, 'L0_xattn_Wq': _L0_xattn_in['Wq'], 'L0_xattn_Wk': _L0_xattn_in['Wk'], 'L0_xattn_Wv': _L0_xattn_in['Wv'], 'L0_xattn_Wo': _L0_xattn_in['Wo'], 'L0_xattn_bo': _L0_xattn_in['bo'], 'L0_ffn_Wgate': _L0_ffn_in['Wgate'], 'L0_ffn_bgate': _L0_ffn_in['bgate'], 'L0_ffn_W1': _L0_ffn_in['W1'], 'L0_ffn_b1': _L0_ffn_in['b1'], 'L0_ffn_W2': _L0_ffn_in['W2'], 'L0_ffn_b2': _L0_ffn_in['b2'], 'L0_ffn_Wg': _L0_ffn_in['Wg'], 'L0_ffn_bg': _L0_ffn_in['bg'], 'L0_ffn_Wl': _L0_ffn_in['Wl'], 'L0_ffn_bl': _L0_ffn_in['bl'], 'L0_ffn_W3': _L0_ffn_in['W3'], 'L0_ffn_b3': _L0_ffn_in['b3'], 'L1_xattn_Wq': _L1_xattn_in['Wq'], 'L1_xattn_Wkv': _L1_xattn_in['Wkv'], 'L1_xattn_Wo': _L1_xattn_in['Wo'], 'L1_ffn_rhs': _L1_ffn_in['rhs'], 'L2_xattn_Wq': _L2_xattn_in['Wq'], 'L2_xattn_bq': _L2_xattn_in['bq'], 'L2_xattn_Wk': _L2_xattn_in['Wk'], 'L2_xattn_bk': _L2_xattn_in['bk'], 'L2_xattn_Wv': _L2_xattn_in['Wv'], 'L2_xattn_bv': _L2_xattn_in['bv'], 'L2_xattn_Wo': _L2_xattn_in['Wo'], 'L2_xattn_bo': _L2_xattn_in['bo'], 'L2_ffn_w_freq_real': _L2_ffn_in['w_freq_real'], 'L2_ffn_w_freq_imag': _L2_ffn_in['w_freq_imag'], 'L2_ffn_bias': _L2_ffn_in['bias'], 'L3_xattn_ln1_g': _L3_xattn_in['ln1_g'], 'L3_xattn_ln1_b': _L3_xattn_in['ln1_b'], 'L3_xattn_ln2_g': _L3_xattn_in['ln2_g'], 'L3_xattn_ln2_b': _L3_xattn_in['ln2_b'], 'L3_xattn_a1_wq': _L3_xattn_in['a1_wq'], 'L3_xattn_a1_wk': _L3_xattn_in['a1_wk'], 'L3_xattn_a1_wv': _L3_xattn_in['a1_wv'], 'L3_xattn_a1_li1_w': _L3_xattn_in['a1_li1_w'], 'L3_xattn_a1_li1_b': _L3_xattn_in['a1_li1_b'], 'L3_xattn_a1_lnx_g': _L3_xattn_in['a1_lnx_g'], 'L3_xattn_a1_lnx_b': _L3_xattn_in['a1_lnx_b'], 'L3_xattn_a1_lny_g': _L3_xattn_in['a1_lny_g'], 'L3_xattn_a1_lny_b': _L3_xattn_in['a1_lny_b'], 'L3_xattn_a1_ln3_g': _L3_xattn_in['a1_ln3_g'], 'L3_xattn_a1_ln3_b': _L3_xattn_in['a1_ln3_b'], 'L3_xattn_a1_li2_w': _L3_xattn_in['a1_li2_w'], 'L3_xattn_a1_li2_b': _L3_xattn_in['a1_li2_b'], 'L3_xattn_a1_li3_w': _L3_xattn_in['a1_li3_w'], 'L3_xattn_a1_li3_b': _L3_xattn_in['a1_li3_b'], 'L3_xattn_a2_wq': _L3_xattn_in['a2_wq'], 'L3_xattn_a2_wk': _L3_xattn_in['a2_wk'], 'L3_xattn_a2_wv': _L3_xattn_in['a2_wv'], 'L3_xattn_a2_li1_w': _L3_xattn_in['a2_li1_w'], 'L3_xattn_a2_li1_b': _L3_xattn_in['a2_li1_b'], 'L3_xattn_a2_lnx_g': _L3_xattn_in['a2_lnx_g'], 'L3_xattn_a2_lnx_b': _L3_xattn_in['a2_lnx_b'], 'L3_xattn_a2_lny_g': _L3_xattn_in['a2_lny_g'], 'L3_xattn_a2_lny_b': _L3_xattn_in['a2_lny_b'], 'L3_xattn_a2_ln3_g': _L3_xattn_in['a2_ln3_g'], 'L3_xattn_a2_ln3_b': _L3_xattn_in['a2_ln3_b'], 'L3_xattn_a2_li2_w': _L3_xattn_in['a2_li2_w'], 'L3_xattn_a2_li2_b': _L3_xattn_in['a2_li2_b'], 'L3_xattn_a2_li3_w': _L3_xattn_in['a2_li3_w'], 'L3_xattn_a2_li3_b': _L3_xattn_in['a2_li3_b'], 'L3_ffn_router_w': _L3_ffn_in['router_w'], 'L3_ffn_router_b': _L3_ffn_in['router_b'], 'L3_ffn_w1': _L3_ffn_in['w1'], 'L3_ffn_b1': _L3_ffn_in['b1'], 'L3_ffn_w2': _L3_ffn_in['w2'], 'L3_ffn_b2': _L3_ffn_in['b2']}

def reference(x, ctx_512, L0_xattn_Wq, L0_xattn_Wk, L0_xattn_Wv, L0_xattn_Wo, L0_xattn_bo, L0_ffn_Wgate, L0_ffn_bgate, L0_ffn_W1, L0_ffn_b1, L0_ffn_W2, L0_ffn_b2, L0_ffn_Wg, L0_ffn_bg, L0_ffn_Wl, L0_ffn_bl, L0_ffn_W3, L0_ffn_b3, L1_xattn_Wq, L1_xattn_Wkv, L1_xattn_Wo, L1_ffn_rhs, L2_xattn_Wq, L2_xattn_bq, L2_xattn_Wk, L2_xattn_bk, L2_xattn_Wv, L2_xattn_bv, L2_xattn_Wo, L2_xattn_bo, L2_ffn_w_freq_real, L2_ffn_w_freq_imag, L2_ffn_bias, L3_xattn_ln1_g, L3_xattn_ln1_b, L3_xattn_ln2_g, L3_xattn_ln2_b, L3_xattn_a1_wq, L3_xattn_a1_wk, L3_xattn_a1_wv, L3_xattn_a1_li1_w, L3_xattn_a1_li1_b, L3_xattn_a1_lnx_g, L3_xattn_a1_lnx_b, L3_xattn_a1_lny_g, L3_xattn_a1_lny_b, L3_xattn_a1_ln3_g, L3_xattn_a1_ln3_b, L3_xattn_a1_li2_w, L3_xattn_a1_li2_b, L3_xattn_a1_li3_w, L3_xattn_a1_li3_b, L3_xattn_a2_wq, L3_xattn_a2_wk, L3_xattn_a2_wv, L3_xattn_a2_li1_w, L3_xattn_a2_li1_b, L3_xattn_a2_lnx_g, L3_xattn_a2_lnx_b, L3_xattn_a2_lny_g, L3_xattn_a2_lny_b, L3_xattn_a2_ln3_g, L3_xattn_a2_ln3_b, L3_xattn_a2_li2_w, L3_xattn_a2_li2_b, L3_xattn_a2_li3_w, L3_xattn_a2_li3_b, L3_ffn_router_w, L3_ffn_router_b, L3_ffn_w1, L3_ffn_b1, L3_ffn_w2, L3_ffn_b2):
    import jax
    import jax.numpy as jnp

    def _L0_xattn_ref(q, kv, Wq, Wk, Wv, Wo, bo):
        import jax, jax.numpy as jnp
        import numpy as np
        NUM_HEADS = 16
        HEAD_DIM = 64
        Q_DIM = 128
        KV_DIM = 64
        INNER = NUM_HEADS * HEAD_DIM
        B, N, _ = q.shape
        M = kv.shape[1]
        scale = HEAD_DIM ** (-0.5)
        qh = (q @ Wq).reshape(B, N, NUM_HEADS, HEAD_DIM).transpose(0, 2, 1, 3)
        kh = (kv @ Wk).reshape(B, M, NUM_HEADS, HEAD_DIM).transpose(0, 2, 1, 3)
        vh = (kv @ Wv).reshape(B, M, NUM_HEADS, HEAD_DIM).transpose(0, 2, 1, 3)
        scores = jnp.einsum('bhnd,bhmd->bhnm', qh, kh) * scale
        attn = jax.nn.softmax(scores, axis=-1)
        out = jnp.einsum('bhnm,bhmd->bhnd', attn, vh)
        out = out.transpose(0, 2, 1, 3).reshape(B, N, INNER)
        return out @ Wo + bo

    def _L0_ffn_ref(x, Wgate, bgate, W1, b1, W2, b2, Wg, bg, Wl, bl, W3, b3):
        import jax, jax.numpy as jnp
        import numpy as np
        E, H, F, K = (8, 128, 256, 2)
        B, S = (2, 256)
        gout = x @ Wgate + bgate
        topv, topi = jax.lax.top_k(gout, K)
        topw = jax.nn.softmax(topv, axis=-1)
        combine = jnp.sum(jax.nn.one_hot(topi, E, dtype=x.dtype) * topw[..., None], axis=-2)
        x1 = jnp.einsum('bsh,ehf->bsef', x, W1) + b1
        x2 = jnp.einsum('bsh,ehf->bsef', x, W2) + b2
        z = x1 * x2
        g = jnp.einsum('bsef,efg->bseg', z, Wg) + bg
        o = g * jax.nn.sigmoid(g) * (jnp.einsum('bsef,efg->bseg', z, Wl) + bl)
        y = jnp.einsum('bsef,efh->bseh', o, W3) + b3
        return jnp.einsum('bse,bseh->bsh', combine, y)

    def _L1_xattn_ref(x, z, Wq, Wkv, Wo):
        import jax, jax.numpy as jnp
        import numpy as np
        DIM = 128
        LATENT_DIM = 64
        NUM_HEADS = 16
        HEAD_DIM = DIM // NUM_HEADS
        SCALE = HEAD_DIM ** (-0.5)
        B, xN, _ = x.shape
        _, zN, _ = z.shape
        Q = (x @ Wq.T).reshape(B, xN, NUM_HEADS, HEAD_DIM)
        KV = (z @ Wkv.T).reshape(B, zN, 2, NUM_HEADS, HEAD_DIM)
        K = KV[:, :, 0]
        V = KV[:, :, 1]
        attn = jnp.einsum('bqhd,bkhd->bhqk', Q, K) * SCALE
        attn = jax.nn.softmax(attn, axis=-1)
        O = jnp.einsum('bhqk,bkhd->bqhd', attn, V).reshape(B, xN, DIM)
        return O @ Wo.T

    def _L1_ffn_ref(lhs, rhs):
        import jax, jax.numpy as jnp
        import numpy as np
        INT8_MAX = 127.0

        def _absmax_scale(x, axes):
            amax = jnp.max(jnp.abs(x), axis=axes, keepdims=True)
            return jnp.maximum(amax, 1e-12) / INT8_MAX
        lhs_scale = _absmax_scale(lhs, (2,))
        rhs_scale = _absmax_scale(rhs, (0,))
        q_lhs = jnp.clip(jnp.round(lhs / lhs_scale), -INT8_MAX, INT8_MAX).astype(jnp.int8)
        q_rhs = jnp.clip(jnp.round(rhs / rhs_scale), -INT8_MAX, INT8_MAX).astype(jnp.int8)
        acc = jax.lax.dot_general(q_lhs, q_rhs, (((2,), (0,)), ((), ())), preferred_element_type=jnp.int32)
        return acc.astype(jnp.float32) * lhs_scale * rhs_scale

    def _L2_xattn_ref(q, k, v, Wq, bq, Wk, bk, Wv, bv, Wo, bo):
        import jax, jax.numpy as jnp
        import numpy as np
        HEADS = 16
        D_MODEL = 128
        IMG_MODEL = 64
        D_K = D_MODEL // HEADS
        B, LQ, _ = q.shape
        LKV = k.shape[1]
        qh = (q @ Wq + bq).reshape(B, LQ, HEADS, D_K).transpose(0, 2, 1, 3)
        kh = (k @ Wk + bk).reshape(B, LKV, HEADS, D_K).transpose(0, 2, 1, 3)
        vh = (v @ Wv + bv).reshape(B, LKV, HEADS, D_K).transpose(0, 2, 1, 3)
        scale = 1.0 / np.sqrt(D_K)
        scores = jnp.einsum('bhqd,bhkd->bhqk', qh, kh) * scale
        attn = jax.nn.softmax(scores, axis=-1)
        out = jnp.einsum('bhqk,bhkd->bhqd', attn, vh)
        concat = out.transpose(0, 2, 1, 3).reshape(B, LQ, D_MODEL)
        return concat @ Wo + bo

    def _L2_ffn_ref(x, w_freq_real, w_freq_imag, bias):
        import jax, jax.numpy as jnp
        import numpy as np
        B, N, D = (4, 256, 128)
        SPARSITY = 0.01
        w = jax.lax.complex(w_freq_real, w_freq_imag)
        x_freq = jnp.fft.fft(x, axis=-1)
        y_freq = jnp.einsum('bnd,do->bno', x_freq, w)
        y = jnp.real(jnp.fft.ifft(y_freq, axis=-1))
        return y + bias

    def _L3_xattn_ref(xx, ee, ln1_g, ln1_b, ln2_g, ln2_b, a1_wq, a1_wk, a1_wv, a1_li1_w, a1_li1_b, a1_lnx_g, a1_lnx_b, a1_lny_g, a1_lny_b, a1_ln3_g, a1_ln3_b, a1_li2_w, a1_li2_b, a1_li3_w, a1_li3_b, a2_wq, a2_wk, a2_wv, a2_li1_w, a2_li1_b, a2_lnx_g, a2_lnx_b, a2_lny_g, a2_lny_b, a2_ln3_g, a2_ln3_b, a2_li2_w, a2_li2_b, a2_li3_w, a2_li3_b, training):
        import jax, jax.numpy as jnp
        import numpy as np
        H, D, C1, C2, S, M, B, W = (16, 32, 128, 64, 256, 64, 2, 4)

        def _ln(x, g, b):
            m = jnp.mean(x, -1, keepdims=True)
            v = jnp.var(x, -1, keepdims=True)
            return (x - m) * jax.lax.rsqrt(v + 1e-05) * g + b

        def _mha(x, y, wq, wk, wv, li1_w, li1_b, lnx_g, lnx_b, lny_g, lny_b, ln3_g, ln3_b, li2_w, li2_b, li3_w, li3_b, causal):
            xn = _ln(x, lnx_g, lnx_b)
            yn = _ln(y, lny_g, lny_b)
            q = jnp.einsum('bsc,hcd->bhsd', xn, wq)
            k = jnp.einsum('btc,hcd->bhtd', yn, wk)
            v = jnp.einsum('btc,hcd->bhtd', yn, wv)
            a = jax.nn.softmax(jnp.einsum('bhsd,bhtd->bhst', q, k) * D ** (-0.5), axis=-1)
            if causal:
                s, t = (a.shape[-2], a.shape[-1])
                mask = (jnp.arange(t)[None, :] > jnp.arange(s)[:, None]).astype(a.dtype)
                a = a * mask
            o = jnp.einsum('bhst,bhtd->bhsd', a, v)
            o = o.transpose(0, 2, 1, 3).reshape(x.shape[0], x.shape[1], H * D)
            x_out = x + o @ li1_w + li1_b
            h = jax.nn.gelu(_ln(x_out, ln3_g, ln3_b) @ li2_w + li2_b, approximate=False)
            return x_out + h @ li3_w + li3_b
        x = _ln(xx, ln1_g, ln1_b)
        x = x + _mha(x, x, a1_wq, a1_wk, a1_wv, a1_li1_w, a1_li1_b, a1_lnx_g, a1_lnx_b, a1_lny_g, a1_lny_b, a1_ln3_g, a1_ln3_b, a1_li2_w, a1_li2_b, a1_li3_w, a1_li3_b, causal=True)
        x = _ln(x, ln2_g, ln2_b)
        return x + _mha(x, ee, a2_wq, a2_wk, a2_wv, a2_li1_w, a2_li1_b, a2_lnx_g, a2_lnx_b, a2_lny_g, a2_lny_b, a2_ln3_g, a2_ln3_b, a2_li2_w, a2_li2_b, a2_li3_w, a2_li3_b, causal=False)

    def _L3_ffn_ref(x, router_w, router_b, w1, b1, w2, b2):
        import jax, jax.numpy as jnp
        import numpy as np
        IN_F, OUT_F, BLOCK, NBLK = (128, 512, 32, 16)
        TOPK = NBLK // 4
        x_shape = x.shape
        xf = x.reshape(-1, IN_F)
        n = xf.shape[0]
        prob = jax.nn.softmax(xf @ router_w.T + router_b, axis=-1)
        _, idx = jax.lax.top_k(prob, TOPK)
        mask = jnp.zeros((n, NBLK), bool).at[jnp.arange(n)[:, None], idx].set(True)
        w1b = w1.reshape(NBLK, BLOCK, IN_F)
        b1b = b1.reshape(NBLK, BLOCK)
        h = jnp.einsum('nd,ibd->nib', xf, w1b) + b1b
        h = jnp.where(mask[:, :, None], h, jnp.zeros((), h.dtype))
        h = jax.nn.relu(h)
        w2b = w2.reshape(IN_F, NBLK, BLOCK)
        y = jnp.einsum('nib,dib->nd', jnp.where(mask[:, :, None], h, 0.0), w2b) + b2
        return y.reshape(x_shape)
    x = x + _L0_xattn_ref(_layernorm(x, axis=-1), ctx_512, L0_xattn_Wq, L0_xattn_Wk, L0_xattn_Wv, L0_xattn_Wo, L0_xattn_bo)
    x = x + _L0_ffn_ref(_layernorm(x, axis=-1), L0_ffn_Wgate, L0_ffn_bgate, L0_ffn_W1, L0_ffn_b1, L0_ffn_W2, L0_ffn_b2, L0_ffn_Wg, L0_ffn_bg, L0_ffn_Wl, L0_ffn_bl, L0_ffn_W3, L0_ffn_b3)
    x = x + _L1_xattn_ref(_layernorm(x, axis=-1), ctx_512, L1_xattn_Wq, L1_xattn_Wkv, L1_xattn_Wo)
    x = x + _L1_ffn_ref(_layernorm(x, axis=-1), L1_ffn_rhs)
    x = x + _L2_xattn_ref(_layernorm(x, axis=-1), ctx_512, ctx_512, L2_xattn_Wq, L2_xattn_bq, L2_xattn_Wk, L2_xattn_bk, L2_xattn_Wv, L2_xattn_bv, L2_xattn_Wo, L2_xattn_bo)
    x = x + _L2_ffn_ref(_layernorm(x, axis=-1), L2_ffn_w_freq_real, L2_ffn_w_freq_imag, L2_ffn_bias)
    x = x + _L3_xattn_ref(_layernorm(x, axis=-1), ctx_512, L3_xattn_ln1_g, L3_xattn_ln1_b, L3_xattn_ln2_g, L3_xattn_ln2_b, L3_xattn_a1_wq, L3_xattn_a1_wk, L3_xattn_a1_wv, L3_xattn_a1_li1_w, L3_xattn_a1_li1_b, L3_xattn_a1_lnx_g, L3_xattn_a1_lnx_b, L3_xattn_a1_lny_g, L3_xattn_a1_lny_b, L3_xattn_a1_ln3_g, L3_xattn_a1_ln3_b, L3_xattn_a1_li2_w, L3_xattn_a1_li2_b, L3_xattn_a1_li3_w, L3_xattn_a1_li3_b, L3_xattn_a2_wq, L3_xattn_a2_wk, L3_xattn_a2_wv, L3_xattn_a2_li1_w, L3_xattn_a2_li1_b, L3_xattn_a2_lnx_g, L3_xattn_a2_lnx_b, L3_xattn_a2_lny_g, L3_xattn_a2_lny_b, L3_xattn_a2_ln3_g, L3_xattn_a2_ln3_b, L3_xattn_a2_li2_w, L3_xattn_a2_li2_b, L3_xattn_a2_li3_w, L3_xattn_a2_li3_b, 0)
    x = x + _L3_ffn_ref(_layernorm(x, axis=-1), L3_ffn_router_w, L3_ffn_router_b, L3_ffn_w1, L3_ffn_b1, L3_ffn_w2, L3_ffn_b2)
    return x

_drawn_inputs = setup_inputs


def setup_inputs(seed=0):
    import zlib

    import numpy as np

    out = dict(_drawn_inputs(seed))
    spreads = {'L0_ffn_bgate': (0.0, 0.1),
     'L0_ffn_b1': (0.0, 0.1),
     'L0_ffn_b2': (0.0, 0.1),
     'L0_ffn_bg': (0.0, 0.1),
     'L0_ffn_bl': (0.0, 0.1),
     'L0_ffn_b3': (0.0, 0.1),
     'L2_xattn_bq': (0.0, 0.8),
     'L2_xattn_bk': (0.0, 2.0),
     'L2_xattn_bv': (0.0, 0.8),
     'L2_xattn_bo': (0.0, 0.8),
     'L3_xattn_ln1_g': (1.0, 0.2),
     'L3_xattn_ln1_b': (0.0, 0.573),
     'L3_xattn_ln2_g': (1.0, 0.555),
     'L3_xattn_ln2_b': (0.0, 0.467),
     'L3_xattn_a1_li1_b': (0.0, 0.8),
     'L3_xattn_a1_lnx_g': (1.0, 0.6),
     'L3_xattn_a1_lnx_b': (0.0, 0.8),
     'L3_xattn_a1_lny_g': (1.0, 0.6),
     'L3_xattn_a1_lny_b': (0.0, 0.8),
     'L3_xattn_a1_ln3_g': (1.0, 0.6),
     'L3_xattn_a1_ln3_b': (0.0, 0.8),
     'L3_xattn_a1_li2_b': (0.0, 0.8),
     'L3_xattn_a1_li3_b': (0.0, 0.8),
     'L3_xattn_a2_li1_b': (0.0, 0.8),
     'L3_xattn_a2_lnx_g': (1.0, 0.6),
     'L3_xattn_a2_lnx_b': (0.0, 0.8),
     'L3_xattn_a2_lny_g': (1.0, 0.6),
     'L3_xattn_a2_lny_b': (0.0, 0.8),
     'L3_xattn_a2_ln3_g': (1.0, 0.6),
     'L3_xattn_a2_ln3_b': (0.0, 0.8),
     'L3_xattn_a2_li2_b': (0.0, 0.8),
     'L3_xattn_a2_li3_b': (0.0, 0.8)}
    factors = {'L2_xattn_Wq': 2.876,
     'L2_xattn_Wk': 2.932,
     'L2_ffn_bias': 8.0,
     'L3_xattn_a1_wq': 8.0,
     'L3_xattn_a1_wk': 8.0,
     'L3_xattn_a1_wv': 8.0,
     'L3_xattn_a1_li1_w': 8.0,
     'L3_xattn_a1_li2_w': 8.0,
     'L3_xattn_a1_li3_w': 8.0,
     'L3_xattn_a2_wq': 8.0,
     'L3_xattn_a2_wk': 8.0,
     'L3_xattn_a2_wv': 8.0,
     'L3_xattn_a2_li1_w': 8.0,
     'L3_xattn_a2_li2_w': 8.0,
     'L3_xattn_a2_li3_w': 8.0,
     'L3_ffn_router_w': 7.446,
     'L3_ffn_router_b': 8.0,
     'L3_ffn_w1': 7.768,
     'L3_ffn_b1': 8.0,
     'L3_ffn_w2': 6.451,
     'L3_ffn_b2': 34.951}
    for name, (base, spread) in spreads.items():
        noise = np.random.default_rng([zlib.crc32(name.encode()), seed]).standard_normal(out[name].shape)
        drawn = base * np.exp(spread * noise) if base else spread * noise
        out[name] = jnp.asarray(drawn.astype(out[name].dtype))
    for name, factor in factors.items():
        out[name] = (out[name] * factor).astype(out[name].dtype)
    return out
```

```python
from contextlib import ExitStack

import concourse.bass as bass
from concourse import mybir

F32 = mybir.dt.float32
BF16 = mybir.dt.bfloat16
ALU = mybir.AluOpType
ACT = mybir.ActivationFunctionType
AX = mybir.AxisListType

B, NQ, D = 32, 56, 128
NP = B // 2
M, C = 1500, 64
KT, KP = 12, 125
H = 16
HQ = H * NQ
NJ = HQ // 128
HB = 16
EPS = 1e-5
E, F = 8, 256
RND = 12582912.0


class Prog:

    def __init__(self, new_sem):
        self.new_sem = new_sem
        self.q = {e: [] for e in ("pe", "act", "dve", "pool", "sp")}
        self.pending = {e: [] for e in self.q}
        self.seen = {e: {} for e in self.q}
        self.dma_count = {}
        self.stores = []
        self.era = 0
        self.start_era("in")

    def start_era(self, name):
        self.sem = {e: self.new_sem(f"{name}_{e}") for e in ("pe", "act", "dve", "pool")}
        self.count = {e: 0 for e in self.sem}

    def put(self, e, fn, *waits, sig=True):
        need = []
        if e == "pool" and self.count[e]:
            waits += ([(self.sem[e], self.count[e])],)
        for w in self.pending[e] + list(waits):
            for s, v in (w if isinstance(w, list) else [w]):
                if self.seen[e].get(s.name, 0) < v:
                    self.seen[e][s.name] = v
                    need.append((s, v))
        self.pending[e] = []
        if not sig:
            self.q[e].append((need, fn, None, 0))
            return []
        self.count[e] += 1
        self.q[e].append((need, fn, self.sem[e], 1))
        return [(self.sem[e], self.count[e])]

    def dma(self, sem, out, in_, *waits, e="sp"):
        need = []
        for w in self.pending[e] + list(waits):
            for s, v in w:
                if self.seen[e].get(s.name, 0) < v:
                    self.seen[e][s.name] = v
                    need.append((s, v))
        self.pending[e] = []
        self.dma_count[sem.name] = self.dma_count.get(sem.name, 0) + 16
        self.q[e].append((need, lambda g: g.dma_start(out, in_), sem, 16))
        return [(sem, self.dma_count[sem.name])]

    def all_done(self):
        return [(self.sem[e], self.count[e]) for e in self.sem if self.count[e]]

    def fence(self):
        done = self.all_done()
        for e in self.pending:
            self.pending[e] = self.pending[e] + [done]

    def run(self, e, eng):
        for need, fn, s, n in self.q[e]:
            for w, v in need:
                eng.wait_ge(w, v)
            ins = fn(eng)
            if s is not None:
                ins.then_inc(s, n)


def build(nc, a, out):
    with ExitStack() as ctx:
        def sb(name, shape, dt=F32):
            return ctx.enter_context(nc.sbuf_tensor(name, shape, dt))

        def sem(name):
            return ctx.enter_context(nc.semaphore(name))

        P = Prog(sem)
        put = P.put

        def mm(o, l, r, start, stop, *w, sig=True):
            return put("pe", lambda g: g.matmul(o, l, r, start=start, stop=stop, skip_group_check=True), *w, sig=sig)

        def tr(o, i, idn, *w, sig=True):
            return put("pe", lambda g: g.transpose(o, i, idn), *w, sig=sig)

        def act(o, i, f, *w, bias=0.0, scale=1.0):
            return put("act", lambda g: g.activation(o, i, f, bias=bias, scale=scale), *w)

        def tt(e, o, x, y, op, *w):
            return put(e, lambda g: g.tensor_tensor(o, x, y, op), *w)

        def ts(o, x, s1, s2, op0, op1, *w, e="dve"):
            if s2 is None:
                return put(e, lambda g: g.tensor_scalar(o, x, s1, None, op0), *w)
            return put(e, lambda g: g.tensor_scalar(o, x, s1, s2, op0, op1), *w)

        def stt(o, x, s, y, op0, op1, *w):
            return put("dve", lambda g: g.scalar_tensor_tensor(out=o, in0=x, scalar=s, in1=y, op0=op0, op1=op1), *w)

        def red(o, x, op, *w, negate=False, mag=False):
            return put("dve", lambda g: g.tensor_reduce(o, x, AX.X, op, negate=negate, apply_absolute_value=mag), *w)

        def cp(e, o, x, *w):
            if e == "act":
                return act(o, x, ACT.Copy, *w)
            return put(e, lambda g: g.tensor_copy(o, x), *w)

        def zero(e, o, v=0.0):
            return put(e, lambda g: g.memset(o, v))

        ps = ctx.enter_context(nc.psum_tensor("ps", [128, 4096], F32))

        def bank(k, n=512):
            return ps[:, 512 * k:512 * k + n]

        x = sb("x", [128, NP, D])
        xn = sb("xn", [128, NP, D])
        xT = sb("xT", [128, NP * 128])
        idf = sb("idf", [128, 128])
        idb = sb("idb", [128, 128], BF16)
        one = sb("one", [128, 128])
        crow = sb("crow", [1, 128])
        rowb = sb("rowb", [1, 512])
        st = sb("st", [128, NP, 6])
        mv = sb("mv", [128, NP, 2])
        ve = sb("ve", [128, NP])
        rs = sb("rs", [128, NP])
        mhalf = sb("mhalf", [128, NP])
        small = sb("small", [128, 64])
        big = sb("big", [128, 21504])
        wa = sb("wa", [128, H * 128])
        wb = sb("wb", [128, H * 128])
        wst = sb("wst", [128, 6144])
        Qh = big[:, 0:7168].bitcast(BF16).rearrange("p (b n) -> p b n", b=HB)
        Ql = big[:, 7168:14336].bitcast(BF16).rearrange("p (b n) -> p b n", b=HB)
        O = big[:, 14336:21504].rearrange("p (b j c) -> p b j c", b=HB, j=NJ)
        cTs = sb("cTs", [128, 2 * M])
        cT = [cTs[:, M * i:M * i + M] for i in range(2)]
        cx = sb("cx", [128, 7608])
        cs = [cx[:, 750 * i:750 * i + 750].bitcast(BF16) for i in range(3)]
        chx = [cx[0:67, 2250 + 750 * i:3000 + 750 * i].bitcast(BF16) for i in range(2)]
        cn = [cx[0:KP, 3750 + 768 * i:4518 + 768 * i].rearrange("p (t c) -> p t c", t=KT) for i in range(2)]
        cnb = [cx[0:KP, 5286 + 774 * i:6060 + 774 * i].bitcast(BF16).rearrange("p (t c) -> p t c", t=KT) for i in range(3)]
        pf = [wst[:, HQ * i:HQ * i + HQ] for i in range(3)]
        pl = [wst[:, 2688 + 448 * i:3136 + 448 * i].bitcast(BF16) for i in range(3)]
        raw = [wst[:, 4032 + 903 * i:4935 + 903 * i].rearrange("p (j c) -> p j c", j=NJ) for i in range(2)]
        mx = [sb(f"mx{i}", [128, NJ, 3]) for i in range(2)]
        nm = [sb(f"nm{i}", [128, 3, NJ]) for i in range(2)]
        m3 = [sb(f"m3{i}", [128, NJ, 3], BF16) for i in range(2)]
        rden = [sb(f"rden{i}", [128, NJ]) for i in range(2)]

        s_in = sem("s_in")
        s_w = sem("s_w")
        s_e = [sem("s_e0"), sem("s_e1")]
        s_cT = [sem("s_cT0"), sem("s_cT1")]
        s_cn = [sem("s_cn0"), sem("s_cn1")]
        s_sT = [sem("s_sT0"), sem("s_sT1")]
        s_sn = [sem("s_sn0"), sem("s_sn1")]
        s_out = sem("s_out")

        yT = nc.dram_tensor("ynT", [B, C, M], F32).ap()
        yN = nc.dram_tensor("ynN", [B, KP, KT * C], F32).ap()

        free = [[] for _ in range(8)]
        turn = [0]

        def take():
            k = turn[0] % 8
            turn[0] += 1
            return k, free[k]

        def evac_e(n):
            return "act" if n % 2 else "dve"

        zx = zero("dve", x[:, :, :])
        zm = zero("pool", mhalf[:, :], -0.5)
        zo = zero("pool", one[:, :], 1.0)
        t_in = []
        xv = a["x"].rearrange("(p r) q d -> r q p d", r=2)
        for r in range(2):
            t_in = P.dma(s_in, x[64 * r:64 * r + NQ, :, :], xv[r], zx)
        t_in = P.dma(s_in, idf[:, :], a["ident"])
        cp("pool", idb[:, :], idf[:, :], t_in)
        P.fence()
        for e in ("pe", "dve", "act", "pool"):
            P.pending[e].append(t_in)

        def layernorm(src, dst):
            t = []
            for p in range(NP):
                t = put("dve", lambda g, p=p: g.bn_stats(st[:, p, :], src[:, p, :]))
            for p in range(NP):
                t2 = put("dve", lambda g, p=p: g.bn_aggr(mv[:, p, :], st[:, p, :]), t)
            t = ts(ve[:, :], mv[:, :, 1], EPS, None, ALU.add, None, t2)
            t = tt("pool", rs[:, :], ve[:, :], mhalf[:, :], ALU.pow, t)
            return [ts(dst[:, p, :], src[:, p, :], mv[:, p, 0:1], rs[:, p:p + 1], ALU.subtract, ALU.mult, t)
                    for p in range(NP)]

        def transpose_all(src, ready, *dsts):
            done = []
            for g4 in range(4):
                k, w = take()
                for q in range(4):
                    t = tr(bank(k)[:, 128 * q:128 * q + 128], src[:, 4 * g4 + q, :], idf[:, :],
                           w, ready[4 * g4 + q], sig=(q == 3))
                for dst, g, b in dsts:
                    o = dst[:, 512 * g4:512 * g4 + 512]
                    if g is None:
                        r = cp(evac_e(g4), o, bank(k), t)
                    else:
                        r = ts(o, bank(k), g, b, ALU.mult, ALU.add, t)
                free[k] = r
                done += free[k]
            return done

        def tok8(t, c):
            return t[:, 512 * c:512 * c + 512].rearrange("p (b q) -> p b q", q=64)[:, :, 0:NQ]

        def q8(k):
            return bank(k, 448).rearrange("p (b q) -> p b q", q=NQ)

        def fold(n, nd, wq, wk, wv, wo, dup, ready):
            done = []
            per = 512 // n
            wav = wa[:, :].rearrange("p (h r c) -> p h r c", h=H, r=128 // n)
            for h0 in range(0, H, per):
                k, w = take()
                for h in range(h0, h0 + per):
                    t = mm(bank(k)[:, n * (h - h0):n * (h - h0) + n], wq[0:nd, h, :], wk[0:nd, h, :], True, True,
                           w, ready, sig=(h == h0 + per - 1))
                src = bank(k).rearrange("p (h c) -> p h c", c=n)
                r = []
                for d in range(128 // n if dup else 1):
                    r = cp(evac_e(h0 // per), wav[:, h0:h0 + per, d, :], src, t)
                free[k] = r
                done += r
            for h0 in range(0, H, 4):
                k, w = take()
                for h in range(h0, h0 + 4):
                    t = mm(bank(k)[0:n, 128 * (h - h0):128 * (h - h0) + 128], wv[0:nd, h, :], wo[0:nd, h, :], True, True,
                           w, ready, sig=(h == h0 + 3))
                free[k] = cp(evac_e(h0 // 4), wb[0:n, 128 * h0:128 * h0 + 512], bank(k)[0:n, :], t)
                done += free[k]
            return done

        def load_w(names, ready=[]):
            views, at, t = [], 0, []
            for name in names:
                d, h, n = a[name].shape
                v = wst[0:d, at:at + h * n].rearrange("d (h n) -> d h n", h=h)
                at += h * n
                t = P.dma(s_w, v, a[name], ready)
                views.append(v)
            return views, t

        def rows_in(names):
            at, t, o = 0, [], []
            for name in names:
                n = a[name].shape[1]
                t = P.dma(s_w, rowb[0:1, at:at + n], a[name])
                o.append(rowb[0:1, at:at + n])
                at += n
            return o, t

        wbv = wb[:, :].rearrange("p (h n) -> p h n", h=H)
        wav = wa[:, :].rearrange("p (h n) -> p h n", h=H)

        def cross(name, scale, srcN, srcT, qsrc, add_to, bias=None):
            def project(b0):
                for c in range(HB // 8):
                    for h in range(H):
                        k, w = take()
                        t = mm(bank(k, 448), wav[:, h, :], tok8(qsrc, b0 // 8 + c), True, True, w)
                        o = slice(8 * c, 8 * c + 8), slice(NQ * h, NQ * h + NQ)
                        bq = 0.0 if bias is None else bias[:, h:h + 1]
                        t1 = act(Qh[:, o[0], o[1]], q8(k), ACT.Identity, t, bias=bq)
                        bl = 0.0 if bias is None else bias[0:64, h:h + 1]
                        t2 = stt(Ql[0:64, o[0], o[1]], q8(k)[0:64], bl, Qh[0:64, o[0], o[1]],
                                 ALU.add, ALU.subtract, t, t1)
                        free[k] = t1 + t2

            def attend(b0):
                cT_free, cn_free = [[], []], [[], []]
                cs_use, chx_use = [[], [], []], [[], []]
                cnb_use = [[], [], []]
                t_cT, t_cn, t_cs, t_cl, t_chx, t_cnb, t_cnl = {}, {}, {}, {}, {}, {}, {}
                s1_free = [[], []]
                s2_free = [[], [], []]
                n1, n2 = [0], [0]
                t_max, t_nm, t_m3, t_rows = {}, {}, {}, {}
                pf_free = [[], [], []]
                t_exp, t_pl, t_pv = {}, {}, {}
                pv_free = []
                raw_free = [[], []]

                def load(k):
                    s = k % 2
                    P.dma(s_cT[s], cT[s][0:64, :], srcT[b0 + k], cT_free[s])
                    t_cT[k] = P.dma(s_cT[s], cT[s][64:128, :], srcT[b0 + k], cT_free[s])
                    t_cn[k] = P.dma(s_cn[s], cn[s][:, :, :].rearrange("p t c -> p (t c)"), srcN[b0 + k], cn_free[s])

                def cast_a(k):
                    s, u = k % 2, k % 3
                    t_cs[k] = act(cs[u], cT[s], ACT.Copy, t_cT[k], cs_use[u])
                    t_cl[k] = tt("pool", cs[u][64:128, :], cT[s][64:128, :], cs[u][64:128, :], ALU.subtract, t_cs[k])

                def cast_b(k):
                    s = k % 2
                    t_chx[k] = act(chx[s][0:64, :], cT[s][0:64, :], ACT.Copy, t_cT[k], chx_use[s])
                    cT_free[s] = t_chx[k] + t_cl[k]

                def cast_c(k):
                    s, u = k % 2, k % 3
                    t_cnb[k] = act(cnb[u][:, :, 0:C], cn[s][:, :, :], ACT.Copy, t_cn[k], cnb_use[u])
                    t_cnl[k] = tt("pool", cnb[u][:, :, C + 1:], cn[s][:, :, :], cnb[u][:, :, 0:C], ALU.subtract, t_cnb[k])
                    cn_free[s] = t_cnl[k]

                def chunk(k, n):
                    j, c = n // 3, n % 3
                    s = n1[0] % 2
                    n1[0] += 1
                    t = mm(bank(s, 500), Qh[:, k, 128 * j:128 * j + 128], cs[k % 3][:, 500 * c:500 * c + 500], True, True,
                           s1_free[s], t_cl[k])
                    s1_free[s] = t_max[k] = red(mx[k % 2][:, j, c:c + 1], bank(s, 500), ALU.max, t)

                def maxima(k):
                    s = k % 2
                    q = nm[s]
                    t = red(q[:, 0, :], mx[s][:, :, :], ALU.max, t_max[k], t_m3.get(k - 2, []), negate=True)
                    for n in range(3):
                        t = put("pool", lambda g, n=n: g.tensor_copy(m3[s][:, :, n], q[:, n, :]), t, t_rows.get(k - 2, []))
                        if n < 2:
                            t = tt("pool", q[:, n + 1, :], q[:, n, :], m3[s][:, :, n], ALU.subtract, t)
                    t_m3[k] = t

                def rows(k):
                    done = []
                    for j0, j1 in ((0, 4), (4, NJ)):
                        s = n2[0] % 3
                        n2[0] += 1
                        for j in range(j0, j1):
                            t = mm(bank(2 + s)[64:67, 128 * (j - j0):128 * (j - j0) + 128], m3[k % 2][:, j, :], idb[:, :],
                                   True, True, s2_free[s], t_m3[k], sig=(j == j1 - 1))
                        s2_free[s] = cp("act", Ql[64:67, k, 128 * j0:128 * j1], bank(2 + s)[64:67, 0:128 * (j1 - j0)], t)
                        done += s2_free[s]
                        t_rows[k] = t
                    return done

                t_neg = {}

                def scores(T):
                    k, t = divmod(T, KT)
                    u, r = k % 3, T % 3
                    done = []
                    for hf in range(2):
                        s = n2[0] % 3
                        n2[0] += 1
                        cols = slice(448 * hf, 448 * hf + 448)
                        keys = slice(KP * t, KP * t + KP)
                        mm(bank(2 + s, 448)[0:KP], cs[u][:, keys], Qh[:, k, cols], True, False,
                           s2_free[s], t_cl[k], sig=False)
                        w = mm(bank(2 + s, 448)[0:KP], chx[k % 2][:, keys], Ql[0:67, k, cols], False, True, t_neg[k], t_chx[k])
                        if t == KT - 1:
                            cs_use[u] = chx_use[k % 2] = w
                        s2_free[s] = act(pf[r][0:KP, cols], bank(2 + s, 448)[0:KP], ACT.Exp, w, pf_free[r], scale=scale)
                        done += s2_free[s]
                    t_exp[T] = done

                def rest(T):
                    r = T % 3
                    t_pl[T] = tt("dve", pl[r][0:KP, :], pf[r][0:KP, :], pf[r][0:KP, :].bitcast(BF16)[:, 1::2],
                                 ALU.subtract, t_exp[T], pf_free[r])

                def pv(T):
                    k, t = divmod(T, KT)
                    u, r = k % 3, T % 3
                    ph = pf[r][0:KP, :].bitcast(BF16)[:, 1::2]
                    for j in range(NJ):
                        o = bank(5 + j // 3)
                        at = 129 * (j % 3)
                        cols = slice(128 * j, 128 * j + 128)
                        mm(o[:, at:at + 129], ph[:, cols], cnb[u][:, t, :], t == 0 and j % 3 == 0, False,
                           pv_free, t_pl[T], t_cnl[k], sig=False)
                        w = mm(o[:, at:at + 65], pl[r][0:KP, cols], cnb[u][:, t, 0:65], False, t == KT - 1,
                               sig=(j == NJ - 1))
                    pf_free[r] = w
                    t_pv[T] = w
                    if t == KT - 1:
                        cnb_use[u] = w

                def finish(k):
                    s = k % 2
                    done = []
                    for g in range(3):
                        n = min(3, NJ - 3 * g)
                        done += cp("act", raw[s][:, 3 * g:3 * g + n, :].rearrange("p j c -> p (j c)"),
                                   bank(5 + g, 129 * n), t_pv[KT * k + KT - 1], raw_free[s])
                    pv_free[:] = done
                    t = put("dve", lambda g: g.reciprocal(rden[s][:, :], raw[s][:, :, C]), done, raw_free[s])
                    t1 = tt("pool", O[:, k, :, :], raw[s][:, :, 0:C], raw[s][:, :, C + 1:], ALU.add, done)
                    t2 = tt("pool", O[:, k, :, :], O[:, k, :, :], rden[s][:, :].unsqueeze(2).broadcast_to([128, NJ, C]),
                            ALU.mult, t, t1)
                    raw_free[s] = t2

                for T in range(-26, KT * HB + 3):
                    for k in range(HB):
                        if T == KT * k - 26:
                            load(k)
                        if T == KT * k - 23:
                            cast_a(k)
                        if T == KT * k - 10:
                            cast_b(k)
                        if T == KT * k - 19:
                            cast_c(k)
                        if T == KT * k - 3:
                            maxima(k)
                        if T == KT * k - 2:
                            t_neg[k] = rows(k)
                        if T == KT * k + KT + 2:
                            finish(k)
                    if 0 <= T < KT * HB:
                        scores(T)
                    for k in range(HB):
                        for n in range(21):
                            if T == KT * k - 16 + n * KT // 21:
                                chunk(k, n)
                    if 0 <= T - 1 < KT * HB:
                        rest(T - 1)
                    if 0 <= T - 2 < KT * HB:
                        pv(T - 2)

            def gather(b0):
                oT = [wst[0:64, 0:2048], wst[0:64, 2048:4096]]
                zs = [zero("pool", o) for o in oT]
                o_free = [[], []]
                n = 0
                for pp in range(HB // 2):
                    ob = oT[pp % 2].rearrange("c (h q) -> c h q", h=H)
                    t_o = []
                    for r in range(2):
                        ka = 2 * (n % 3)
                        n += 1
                        w = free[ka] + free[ka + 1]
                        for j in range(NJ):
                            t = tr(ps[0:64, 512 * ka + 128 * j:512 * ka + 128 * j + 128], O[:, 2 * pp + r, j, :], idf[:, :],
                                   w, sig=(j == NJ - 1))
                        e = evac_e(r)
                        t_o += cp(e, ob[:, :, 64 * r:64 * r + NQ],
                                  ps[0:64, 512 * ka:512 * ka + HQ].rearrange("c (h q) -> c h q", h=H),
                                  t, zs[pp % 2], o_free[pp % 2])
                        free[ka] = free[ka + 1] = t_o
                    k = 6 + pp % 2
                    p = b0 // 2 + pp
                    mm(bank(k, 128), one[0:1, :], crow[0:1, :], True, False, free[k], sig=False)
                    for h in range(H):
                        t = mm(bank(k, 128), ob[:, h, :], wbv[0:64, h, :], False, h == H - 1, t_o, sig=(h == H - 1))
                    o_free[pp % 2] = t
                    free[k] = tt("dve", add_to[:, p, :], add_to[:, p, :], bank(k, 128), ALU.add, t)

            for k in range(3):
                if k < 2:
                    zero("pool", chx[k][64:67, :], 1.0)
                zero("pool", cnb[k][:, :, C:C + 1], 1.0)
            for b0 in range(0, B, HB):
                project(b0)
                P.fence()
                attend(b0)
                P.fence()
                for k in range(8):
                    free[k] = []
                gather(b0)
                P.fence()
                for k in range(8):
                    free[k] = []

        def layer(name):
            P.fence()
            P.start_era(name)
            for k in range(8):
                free[k] = []

        ctxN, ctxT = a["ctxN"], a["ctxT"]
        (wq, wk, wv), tw = load_w(["L0q", "L0k", "L0v"])
        wo0 = big[0:64, 0:2048].rearrange("d (h n) -> d h n", h=H)
        P.dma(s_w, wo0, a["L0o"])
        tw = P.dma(s_w, crow[:, :], a["L0bo"])
        n = layernorm(x, xn)
        transpose_all(xn, n, (xT, None, None))
        fold(64, 64, wq, wk, wv, wo0, True, tw)
        layer("L0a")
        cross("L0", 64 ** -0.5, ctxN, ctxT, xT, x)

        gw = wst[:, 4096:4104]
        P.dma(s_w, gw, a["Wgate"])
        P.dma(s_w, crow[0:1, 0:E], a["bgate"])
        tri = wst[:, 4224:4224 + 64].rearrange("p (i j) -> p i j", i=E)
        P.dma(s_w, tri, a["tri8"])
        b3 = wst[0:E, 4352:4480]
        P.dma(s_w, b3, a["b3"])
        ebias = wst[:, 4480:4480 + 64].rearrange("p (e k) -> p e k", e=E)
        tw = P.dma(s_w, ebias, a["ebias"])
        ew = [wst[:, 0:2048], wst[:, 2048:4096]]
        ew3 = [wst[:, 4608:4864], wst[:, 4864:5120]]

        def load_e(e, *w):
            s = e % 2
            P.dma(s_e[s], ew[s], a["ew"][e], *w)
            return P.dma(s_e[s], ew3[s], a["ew3"][e], *w)

        te = {e: load_e(e) for e in range(2)}
        n = layernorm(x, xn)
        t_x = transpose_all(xn, n, (xT, None, None))

        def rank_sel(val, nb, ne, top, tri_, sel, ready, g1, g2):
            vi = val.unsqueeze(3).broadcast_to([128, nb, ne, ne])
            vj = val.unsqueeze(2).broadcast_to([128, nb, ne, ne])
            t = []
            for p in range(nb):
                t1 = tt("dve", g1[:, p], vj[:, p], vi[:, p], ALU.is_ge, ready)
                t2 = tt("dve", g2[:, p], vj[:, p], vi[:, p], ALU.is_gt, ready)
                t1 = tt("dve", g1[:, p], g1[:, p], tri_, ALU.mult, t1)
                t2 = tt("dve", g1[:, p], g1[:, p], g2[:, p], ALU.max, t1, t2)
                t = red(ve_big[:, p * ne:(p + 1) * ne], g1[:, p], ALU.add, t2)
            return ts(sel, ve_big[:, 0:nb * ne].rearrange("p (b e) -> p b e", b=nb), float(top), None, ALU.is_lt, None, t)

        ve_big = big[:, 12288:12544]
        g1 = big[:, 8192:9216].rearrange("p (b i j) -> p b i j", b=NP, i=E)
        g2 = big[:, 9216:10240].rearrange("p (b i j) -> p b i j", b=NP, i=E)
        lg = big[:, 12544:12672].rearrange("p (b e) -> p b e", b=NP)
        sel = big[:, 12672:12800].rearrange("p (b e) -> p b e", b=NP)
        comb = big[:, 12800:12928].rearrange("p (b e) -> p b e", b=NP)
        combT = big[0:E, 13000:13000 + 2048]
        k, w = take()
        for p in range(NP):
            mm(bank(k)[:, E * p:E * p + E], xT[:, 128 * p:128 * p + 128], gw, True, False, w, tw, t_x, sig=False)
            t = mm(bank(k)[:, E * p:E * p + E], one[0:1, :], crow[0:1, 0:E], False, True)
        t = cp("dve", lg, bank(k, 128).rearrange("p (b e) -> p b e", b=NP), t)
        free[k] = t
        t_s = rank_sel(lg, NP, E, 2, tri, sel, t, g1, g2)
        t1 = red(small[:, 0:NP], lg, ALU.max, t)
        t1 = tt("dve", lg, lg, small[:, 0:NP].unsqueeze(2).broadcast_to([128, NP, E]), ALU.subtract, t1, t_s)
        t1 = act(lg, lg, ACT.Exp, t1)
        t1 = tt("dve", comb, lg, sel, ALU.mult, t1, t_s)
        t2 = red(small[:, 16:16 + NP], comb, ALU.add, t1)
        t2 = put("dve", lambda g: g.reciprocal(small[:, 32:32 + NP], small[:, 16:16 + NP]), t2)
        t_c = tt("dve", comb, comb, small[:, 32:32 + NP].unsqueeze(2).broadcast_to([128, NP, E]), ALU.mult, t2)
        for g4 in range(4):
            k, w = take()
            for q in range(4):
                t = tr(bank(k)[0:E, 128 * q:128 * q + 128], comb[:, 4 * g4 + q, :], idf[:, :], w, t_c, sig=(q == 3))
            free[k] = cp("act", combT[:, 512 * g4:512 * g4 + 512], bank(k)[0:E, :], t)
        t_ct = free[k]
        t_acc = {}
        for p in range(NP):
            k, w = take()
            t = mm(bank(k, 128), combT[:, 128 * p:128 * p + 128], b3, True, True, w, t_ct)
            free[k] = t_acc[p] = tt("dve", x[:, p, :], x[:, p, :], bank(k, 128), ALU.add, t)
        z1 = [big[:, 0:896], big[:, 896:1792]]
        zz = [big[:, 1792:2688], big[:, 2688:3584]]
        sg = [big[:, 3584:4480], big[:, 4480:5376]]
        oo = [big[:, 5376:6400], big[:, 6400:7424]]
        t_z = [zero("pool", o) for o in oo]
        z_use, o_use = [[], []], [[], []]
        step = 0
        for e in range(E):
            s = e % 2
            w1 = ew[s][:, 0:256]
            w2 = ew[s][:, 256:512]
            wg = ew[s][:, 512:1024].rearrange("p (k n) -> p k n", k=2)
            wl = ew[s][:, 1024:1536].rearrange("p (k n) -> p k n", k=2)
            w3 = ew3[s].rearrange("p (k n) -> p k n", k=2)
            for c in range(4):
                u = step % 2
                step += 1
                t_zf = []
                for f in range(2):
                    cols = slice(128 * f, 128 * f + 128)
                    half = slice(448 * f, 448 * f + 448)
                    k1, w = take()
                    t1 = mm(bank(k1, 448), w1[:, cols], tok8(xT, c), True, True, w, te[e])
                    k2, w = take()
                    t2 = mm(bank(k2, 448), w2[:, cols], tok8(xT, c), True, True, w)
                    free[k1] = act(z1[u][:, half], bank(k1, 448), ACT.Identity, t1, z_use[u], bias=ebias[:, e, f:f + 1])
                    free[k2] = stt(zz[u][:, half], bank(k2, 448), ebias[:, e, 2 + f:3 + f], z1[u][:, half],
                                   ALU.add, ALU.mult, t2, free[k1], z_use[u])
                    t_zf += free[k2]
                t_o = []
                for f in range(2):
                    cols = slice(128 * f, 128 * f + 128)
                    half = slice(448 * f, 448 * f + 448)
                    k1, w = take()
                    for i in range(2):
                        t1 = mm(bank(k1, 448), wg[:, i, cols], zz[u][:, 448 * i:448 * i + 448], i == 0, i == 1,
                                w, t_zf[0:i + 1], sig=(i == 1))
                    k2, w = take()
                    for i in range(2):
                        t2 = mm(bank(k2, 448), wl[:, i, cols], zz[u][:, 448 * i:448 * i + 448], i == 0, i == 1,
                                w, sig=(i == 1))
                    ta = act(sg[u][:, half], bank(k1, 448), ACT.Sigmoid, t1, o_use[u], bias=ebias[:, e, 4 + f:5 + f])
                    tb = stt(sg[u][:, half], bank(k1, 448), ebias[:, e, 4 + f:5 + f], sg[u][:, half], ALU.add, ALU.mult, ta)
                    free[k1] = ta + tb
                    ov = oo[u][:, 512 * f:512 * f + 512].rearrange("p (b q) -> p b q", q=64)[:, :, 0:NQ]
                    free[k2] = stt(ov, q8(k2), ebias[:, e, 6 + f:7 + f], sg[u][:, half].rearrange("p (b q) -> p b q", q=NQ),
                                   ALU.add, ALU.mult, t2, tb, o_use[u], t_z[u])
                    t_o += free[k2]
                z_use[u] = t2
                k, w = take()
                r = []
                for q in range(4):
                    p = 4 * c + q
                    for i in range(2):
                        t = mm(bank(k)[:, 128 * q:128 * q + 128], oo[u][:, 512 * i + 128 * q:512 * i + 128 * q + 128],
                               w3[:, i, :], i == 0, i == 1, w, t_o, sig=(i == 1))
                    if q == 3:
                        o_use[u] = t
                        te_use = t
                for q in range(4):
                    p = 4 * c + q
                    t_acc[p] = stt(x[:, p, :], bank(k)[:, 128 * q:128 * q + 128], comb[:, p, e:e + 1], x[:, p, :],
                                   ALU.mult, ALU.add, o_use[u], t_acc[p])
                    r += t_acc[p]
                free[k] = r
            if e + 2 < E:
                te[e + 2] = load_e(e + 2, te_use)
        layer("L1a")

        (wq, wk, wv), tw = load_w(["L1q", "L1k", "L1v"])
        wo1 = big[0:8, 0:2048].rearrange("d (h n) -> d h n", h=H)
        tw = P.dma(s_w, wo1, a["L1o"])
        t0 = zero("pool", crow[:, :])
        n = layernorm(x, xn)
        transpose_all(xn, n, (xT, None, None))
        fold(64, 8, wq, wk, wv, wo1, True, tw)
        layer("L1b")
        cross("L1", 8 ** -0.5, ctxN, ctxT, xT, x)

        rT = wst[:, 0:128]
        tw = P.dma(s_w, rT, a["rhsT"])
        n = layernorm(x, xn)
        qf = big[:, 0:2048].rearrange("p (b d) -> p b d", b=NP)
        xq = big[:, 2048:3072].bitcast(BF16)
        rq = wst[:, 128:256]
        rqb = wst[:, 256:320].bitcast(BF16)
        dg = wst[:, 384:512]
        rsb = wst[:, 512:640]
        amax = small[:, 0:17]
        scl = small[:, 17:34]
        inv = small[:, 34:51]
        t1 = red(amax[:, 0:NP], xn[:, :, :], ALU.max, sum(n, []), mag=True)
        t2 = red(amax[:, 16:17], rT, ALU.max, tw, mag=True)
        t = ts(scl, amax, 1e-12, 1.0 / 127.0, ALU.max, ALU.mult, t1, t2)
        t_s = put("dve", lambda g: g.reciprocal(inv, scl), t)

        def quantize(o, i, s, *w):
            t = ts(o, i, s, RND, ALU.mult, ALU.add, *w)
            t = ts(o, o, -RND, 127.0, ALU.add, ALU.min, t)
            return ts(o, o, -127.0, None, ALU.max, None, t)

        n = [quantize(qf[:, p, :], xn[:, p, :], inv[:, p:p + 1], t_s) for p in range(NP)]
        t_x = transpose_all(qf, n, (xq, None, None))
        t = quantize(rq, rT, inv[:, 16:17], t_s, tw)
        k, w = take()
        t = tr(bank(k, 128), rq, idf[:, :], w, t)
        t_r = cp("act", rqb, bank(k, 128), t)
        free[k] = t_r
        t = ts(dg, idf[:, :], scl[:, 16:17], None, ALU.mult, None, t_s)
        k, w = take()
        t = mm(bank(k, 128), one[:, :], dg, True, True, w, t)
        t_b = cp("act", rsb, bank(k, 128), t)
        free[k] = t_b
        for p in range(NP):
            k, w = take()
            t = mm(bank(k, 128), xq[:, 128 * p:128 * p + 128], rqb, True, True, w, t_x, t_r)
            free[k] = stt(qf[:, p, :], bank(k, 128), scl[:, p:p + 1], rsb, ALU.mult, ALU.mult, t, t_b)
            tt("dve", x[:, p, :], x[:, p, :], qf[:, p, :], ALU.add, free[k])
        layer("L2a")

        (wq, wk, wv), tw = load_w(["L2q", "L2k", "L2v"])
        wo2 = big[0:8, 0:2048].rearrange("d (h n) -> d h n", h=H)
        P.dma(s_w, wo2, a["L2o"])
        bqv = big[0:8, 2048:2080].rearrange("d (k h) -> d k h", k=2)
        P.dma(s_w, bqv, a["L2b"])
        (bo2,), tw = rows_in(["L2bo"])
        n = layernorm(x, xn)
        transpose_all(xn, n, (xT, None, None))
        fold(64, 8, wq, wk, wv, wo2, True, tw)
        k, w = take()
        for h in range(H):
            for r in range(2):
                t = mm(bank(k)[64 * r:64 * r + 64, h:h + 1], wk[0:8, h, :], bqv[:, 0, h:h + 1], True, True, w, tw)
        qbias = small[:, 0:H]
        free[k] = cp("dve", qbias, bank(k, H), t)
        k, w = take()
        mm(bank(k, 128)[0:1], one[0:1, 0:1], bo2, True, False, w, sig=False)
        for h in range(H):
            t = mm(bank(k, 128)[0:1], bqv[:, 1, h:h + 1], wo2[:, h, :], False, h == H - 1)
        free[k] = cp("dve", crow[:, :], bank(k, 128)[0:1], t)
        layer("L2b")
        cross("L2", 8 ** -0.5, ctxN, ctxT, xT, x, bias=qbias)

        dft = wst[:, 0:384].rearrange("p (k n) -> p k n", k=3)
        P.dma(s_w, dft, a["dft"])
        wf = wst[:, 384:640].rearrange("p (k n) -> p k n", k=2)
        P.dma(s_w, wf, a["wfreq"])
        tw = P.dma(s_w, crow[:, :], a["L2bias"])
        n = layernorm(x, xn)
        t_x = transpose_all(xn, n, (xT, None, None))
        tq = wst[:, 640:896].rearrange("p (k n) -> p k n", k=2)
        mat = wst[:, 896:1024]
        cosm, sinm, nsin = dft[:, 0, :], dft[:, 1, :], dft[:, 2, :]
        k, w = take()
        mm(bank(k, 128), wf[:, 0, :], cosm, True, False, w, tw)
        mm(bank(k, 128), wf[:, 1, :], sinm, False, True)
        mm(bank(k)[:, 128:256], wf[:, 0, :], sinm, True, False)
        nw = ts(wst[:, 1024:1152], wf[:, 1, :], -1.0, None, ALU.mult, None, tw)
        t = mm(bank(k)[:, 128:256], wst[:, 1024:1152], cosm, False, True, nw)
        t = ts(tq, bank(k, 256).rearrange("p (k n) -> p k n", k=2), 1.0 / 128.0, None, ALU.mult, None, t)
        free[k] = t
        k, w = take()
        mm(bank(k, 128), tq[:, 0, :], cosm, True, False, w, t)
        t = mm(bank(k, 128), tq[:, 1, :], sinm, False, True)
        free[k] = t_m = cp("act", mat, bank(k, 128), t)
        for p in range(NP):
            k, w = take()
            mm(bank(k, 128), one[0:1, :], crow[:, :], True, False, w, tw, sig=False)
            t = mm(bank(k, 128), xT[:, 128 * p:128 * p + 128], mat, False, True, t_x, t_m)
            free[k] = tt("dve", x[:, p, :], x[:, p, :], bank(k, 128), ALU.add, t)
        layer("L3n")

        bc = wst[:, 0:256].rearrange("p (k c) -> p k c", k=4)[:, 0:2, :]
        bcx = [wst[:, 0:64], wst[:, 64:128]]
        P.dma(s_w, bcx[0], a["a2lyg"])
        tw = P.dma(s_w, bcx[1], a["a2lyb"])
        ns = [big[0:KP, 4096 * i:4096 * i + 768].rearrange("p (t c) -> p t c", c=C) for i in range(2)]
        nsq = [big[0:KP, 4096 * i + 768:4096 * i + 1536].rearrange("p (t c) -> p t c", c=C) for i in range(2)]
        nT = [big[0:64, 4096 * i + 1536:4096 * i + 1536 + M] for i in range(2)]
        nst = [big[0:KP, 4096 * i + 3072:4096 * i + 3072 + 64].rearrange("p (k t) -> p k t", k=4)[:, :, 0:KT] for i in range(2)]
        cn_free, sn, sT, n_use = [[], []], [[], []], [[], []], [[], []]
        for k in range(8):
            free[k] = []
        mh12 = mhalf[0:KP, 0:KT]
        for b in range(B):
            s = b % 2
            t_l = P.dma(s_cn[s], cn[s][:, :, :].rearrange("p t c -> p (t c)"), ctxN[b], cn_free[s])
            v, v2, q = ns[s], nsq[s], nst[s]
            t = red(q[:, 0, :], cn[s][:, :, :], ALU.add, t_l)
            t = ts(q[:, 1, :], q[:, 0, :], -1.0 / C, None, ALU.mult, None, t)
            t_v = tt("dve", v, cn[s][:, :, :], q[:, 1, :].unsqueeze(2).broadcast_to([KP, KT, C]), ALU.add, t, sn[s], n_use[s])
            cn_free[s] = t_v
            t = act(v2, v, ACT.Square, t_v)
            t = red(q[:, 2, :], v2, ALU.add, t)
            t = ts(q[:, 2, :], q[:, 2, :], 1.0 / C, EPS, ALU.mult, ALU.add, t)
            t = tt("pool", q[:, 3, :], q[:, 2, :], mh12, ALU.pow, t)
            t = tt("pool", v, v, q[:, 3, :].unsqueeze(2).broadcast_to([KP, KT, C]), ALU.mult, t)
            t = tt("pool", v, v, bcx[0][0:KP].unsqueeze(1).broadcast_to([KP, KT, C]), ALU.mult, t, tw)
            t = tt("pool", v, v, bcx[1][0:KP].unsqueeze(1).broadcast_to([KP, KT, C]), ALU.add, t)
            sn[s] = P.dma(s_sn[s], yN[b], v.rearrange("p t c -> p (t c)"), t)
            kb = 4 * s
            for i in range(KT):
                o = ps[0:64, 512 * kb + 512 * (i // 4) + KP * (i % 4):512 * kb + 512 * (i // 4) + KP * (i % 4) + KP]
                t_t = tr(o, v[:, i, :], idf[0:KP, 0:KP], t, free[kb], sig=(i == KT - 1))
            n_use[s] = t_t
            src = ps[0:64, 512 * kb:512 * kb + 1536].rearrange("c (g n) -> c g n", g=3)[:, :, 0:500]
            free[kb] = cp("act", nT[s].rearrange("c (g n) -> c g n", g=3), src, t_t, sT[s])
            sT[s] = P.dma(s_sT[s], yT[b], nT[s], free[kb])
        stored = sum(sn + sT, [])
        P.stores = stored
        layer("L3a")
        for e in ("sp", "act", "pool", "dve"):
            P.pending[e].append(stored)

        def load_v(name, tile):
            return P.dma(s_w, tile, a[name])

        vec = sb("vec", [128, 32])
        xn2 = sb("xn2", [128, NP, D])
        load_v("L3vec", vec[:, :])
        gb = cx[:, 2048:2816].rearrange("p (k n) -> p k n", k=6)
        tw = load_v("L3bc", gb)
        Lx = cx[:, 0:2048].rearrange("p (b d) -> p b d", b=NP)
        yb = xn
        yTt = cTs[:, 0:2048]

        def affine(buf, g, b, ready):
            done = []
            for p in range(NP):
                t = tt("pool", buf[:, p, :], buf[:, p, :], g, ALU.mult, ready[p], tw)
                done.append(tt("pool", buf[:, p, :], buf[:, p, :], b, ALU.add, t))
            return done

        def mlp(src, dst, v0, l2, l3, brow, twm):
            n = layernorm(src, xn)
            t_x = transpose_all(xn, n, (xT, vec[:, v0:v0 + 1], vec[:, v0 + 1:v0 + 2]))
            hid = [big[:, 0:2048], big[:, 2048:4096]]
            zs = [zero("pool", h) for h in hid]
            use = [[], []]
            for c in range(4):
                u = c % 2
                hv = hid[u].rearrange("p (m n) -> p m n", m=4)
                t_h = []
                for m in range(4):
                    k, w = take()
                    t = mm(bank(k, 448), l2[:, m, :], tok8(xT, c), True, True, w, t_x, twm)
                    free[k] = act(hv[:, m, :].rearrange("p (b q) -> p b q", q=64)[:, :, 0:NQ], q8(k), ACT.Gelu,
                                  t, use[u], zs[u], bias=vec[:, v0 + 2 + m:v0 + 3 + m])
                    t_h += free[k]
                for q in range(4):
                    p = 4 * c + q
                    k, w = take()
                    mm(bank(k, 128), one[0:1, :], brow, True, False, w, sig=False)
                    for m in range(4):
                        t = mm(bank(k, 128), hv[:, m, 128 * q:128 * q + 128], l3[:, m, :], False, m == 3, t_h)
                    use[u] = t
                    free[k] = tt("dve", dst[:, p, :], dst[:, p, :], bank(k, 128), ALU.add, t)

        (wq, wk, wv), _ = load_w(["a1q", "a1k", "a1v"])
        woa = big[0:32, 0:2048].rearrange("d (h n) -> d h n", h=H)
        P.dma(s_w, woa, a["a1o"])
        (a1b1, a1b3, a2b1, a2b3), tw = rows_in(["a1b1", "a1b3", "a2b1", "a2b3"])
        for e in ("dve", "pool", "pe"):
            P.pending[e].append(tw)
        n = layernorm(x, xn)
        P.fence()
        n = layernorm(xn, Lx)
        n = affine(Lx, gb[:, 0, :], gb[:, 1, :], n)
        P.fence()
        n = layernorm(Lx, xn)
        t_x = transpose_all(xn, n, (xT, vec[:, 0:1], vec[:, 1:2]), (yTt, vec[:, 2:3], vec[:, 3:4]))
        fold(128, 32, wq, wk, wv, woa, False, tw)
        P.fence()
        for k in range(8):
            free[k] = []
        affine(yb, gb[:, 2, :], gb[:, 3, :], [[]] * NP)
        maskt = wst[:, 0:392].rearrange("p (j t) -> p j t", j=NJ)
        tw = P.dma(s_w, maskt, a["mask"])
        P.fence()
        P.pending["dve"].append(tw)

        Q1 = big[:, 0:14336].rearrange("p (b n) -> p b n", b=HB)
        sE = [big[:, 14336 + 400 * i:14336 + 400 * i + 392].rearrange("p (j t) -> p j t", j=NJ) for i in range(2)]
        AT = [big[:, 15200 + 896 * i:15200 + 896 * i + 896] for i in range(2)]
        OT = [big[:, 17024 + 2048 * i:17024 + 2048 * i + 2048].rearrange("c (h q) -> c h q", h=H) for i in range(2)]
        zs = [zero("pool", o) for o in OT]
        OT_use = [[], []]
        for b0 in range(0, B, HB):
            t_q = []
            for c in range(HB // 8):
                for h in range(H):
                    k, w = take()
                    t = mm(bank(k, 448), wav[:, h, :], tok8(xT, b0 // 8 + c), True, True, w)
                    free[k] = cp(evac_e(h), Q1[:, 8 * c:8 * c + 8, NQ * h:NQ * h + NQ], q8(k), t)
                    t_q += free[k]
            P.fence()
            for k in range(8):
                free[k] = []
            sE_use, AT_use, t_a, t_ot = [[], []], [[], []], {}, {}
            o2_free, t2_free = [], []

            def soft(i):
                u = i % 2
                b = b0 + i
                v = small[:, 32 * u:32 * u + 28].rearrange("p (k j) -> p k j", k=4)
                for j in range(NJ):
                    t = mm(bank(u)[:, NQ * j:NQ * j + NQ], Q1[:, i, 128 * j:128 * j + 128], yTt[:, 64 * b:64 * b + NQ],
                           True, True, free[u], sig=(j == NJ - 1))
                pv = bank(u, 392).rearrange("p (j t) -> p j t", j=NJ)
                t1 = red(v[:, 0, :], pv, ALU.max, t)
                t1 = tt("dve", sE[u], pv, v[:, 0, :].unsqueeze(2).broadcast_to([128, NJ, NQ]), ALU.subtract, t1, sE_use[u])
                free[u] = t1
                t1 = act(sE[u], sE[u], ACT.Exp, t1, scale=32 ** -0.5)
                t2 = red(v[:, 1, :], sE[u], ALU.add, t1)
                t2 = put("dve", lambda g: g.reciprocal(v[:, 2, :], v[:, 1, :]), t2)
                t1 = tt("dve", sE[u], sE[u], maskt, ALU.mult, t1, t2)
                t_a[i] = tt("dve", sE[u], sE[u], v[:, 2, :].unsqueeze(2).broadcast_to([128, NJ, NQ]), ALU.mult, t1, t2)

            def apply(i):
                u, r = i % 2, i % 2
                pp = i // 2
                p = (b0 + i) // 2
                for j in range(NJ):
                    t = tr(ps[0:NQ, 1024 + 128 * j:1024 + 128 * j + 128], sE[u][:, j, :], idf[:, :], t2_free, t_a[i],
                           sig=(j == NJ - 1))
                sE_use[u] = t
                rows = slice(64 * r, 64 * r + NQ)
                t = cp("act", AT[u][rows, :], ps[0:NQ, 1024:1024 + HQ], t, AT_use[u])
                t2_free[:] = t
                for hf in range(2):
                    tm = mm(bank(4 + hf, 448), yb[rows, p, :], AT[u][rows, 448 * hf:448 * hf + 448], True, True,
                            t, o2_free, sig=(hf == 1))
                AT_use[u] = tm
                done = []
                for hf in range(2):
                    done += cp(evac_e(hf), OT[pp % 2][:, 8 * hf:8 * hf + 8, 64 * r:64 * r + NQ], q8(4 + hf), tm,
                               OT_use[pp % 2], zs[pp % 2])
                o2_free[:] = done
                t_ot[i] = done
                if r == 1:
                    k = 6 + pp % 2
                    mm(bank(k, 128), one[0:1, :], a1b1, True, False, free[k], sig=False)
                    for h in range(H):
                        t = mm(bank(k, 128), OT[pp % 2][:, h, :], wbv[:, h, :], False, h == H - 1,
                               t_ot[i], t_ot[i - 1], sig=(h == H - 1))
                    OT_use[pp % 2] = t
                    free[k] = stt(xn2[:, p, :], Lx[:, p, :], 1.0, bank(k, 128), ALU.mult, ALU.add, t)

            soft(0)
            for i in range(HB):
                if i + 1 < HB:
                    soft(i + 1)
                apply(i)
            P.fence()
            for k in range(8):
                free[k] = []
        l2 = wst[:, 0:512].rearrange("p (m n) -> p m n", m=4)
        l3 = wst[:, 512:1024].rearrange("p (m n) -> p m n", m=4)
        P.dma(s_w, l2, a["a1l2"])
        tw = P.dma(s_w, l3, a["a1l3"])
        for p in range(NP):
            t = tt("pool", Lx[:, p, :], Lx[:, p, :], xn2[:, p, :], ALU.add)
        P.pending["dve"].append(t)
        mlp(xn2, Lx, 4, l2, l3, a1b3, tw)
        layer("L3f")

        (wq, wk, wv), tw = load_w(["a2q", "a2k", "a2v"])
        woa = big[0:32, 0:2048].rearrange("d (h n) -> d h n", h=H)
        tw = P.dma(s_w, woa, a["a2o"])
        n = layernorm(Lx, xn2)
        n = affine(xn2, gb[:, 4, :], gb[:, 5, :], n)
        P.fence()
        for p in range(NP):
            tt("pool", x[:, p, :], x[:, p, :], xn2[:, p, :], ALU.add)
        cp("act", crow[:, :], a2b1)
        n = layernorm(xn2, xn)
        transpose_all(xn, n, (xT, vec[:, 10:11], vec[:, 11:12]))
        fold(64, 32, wq, wk, wv, woa, True, tw)
        layer("L3h")
        cross("L3", 32 ** -0.5, yN, yT, xT, xn2)
        l2 = wst[:, 0:512].rearrange("p (m n) -> p m n", m=4)
        l3 = wst[:, 512:1024].rearrange("p (m n) -> p m n", m=4)
        P.dma(s_w, l2, a["a2l2"])
        tw = P.dma(s_w, l3, a["a2l3"])
        for p in range(NP):
            t = tt("pool", x[:, p, :], x[:, p, :], xn2[:, p, :], ALU.add)
        P.pending["dve"].append(t)
        mlp(xn2, x, 12, l2, l3, a2b3, tw)
        layer("L4")

        rw = wst[:, 0:16]
        P.dma(s_w, rw, a["routerT"])
        f1 = wst[:, 128:640].rearrange("p (m n) -> p m n", m=4)
        P.dma(s_w, f1, a["w1T"])
        f2 = wst[:, 640:1152].rearrange("p (m n) -> p m n", m=4)
        P.dma(s_w, f2, a["w2T"])
        tri = wst[:, 1152:1152 + 256].rearrange("p (i j) -> p i j", i=16)
        P.dma(s_w, tri, a["tri16"])
        spread = wst[0:16, 1408:1920].rearrange("p (m n) -> p m n", m=4)
        P.dma(s_w, spread, a["spread"])
        fb = wst[:, 1920:1924]
        P.dma(s_w, fb, a["f1b"])
        P.dma(s_w, crow[:, :], a["f2b"])
        rbr = rowb[0:1, 0:16]
        tw = P.dma(s_w, rbr, a["routerb"])
        n = layernorm(x, xn)
        t_x = transpose_all(xn, n, (xT, None, None))
        ve_big = big[:, 12288:12544]
        g1 = big[:, 0:4096].rearrange("p (b i j) -> p b i j", b=NP, i=16)
        g2 = big[:, 4096:8192].rearrange("p (b i j) -> p b i j", b=NP, i=16)
        lg = big[:, 12544:12800].rearrange("p (b e) -> p b e", b=NP)
        sel = big[:, 12800:13056].rearrange("p (b e) -> p b e", b=NP)
        selT = big[0:16, 13056:13056 + 2048]
        k, w = take()
        for p in range(NP):
            mm(bank(k)[:, 16 * p:16 * p + 16], xT[:, 128 * p:128 * p + 128], rw, True, False, w, tw, t_x, sig=False)
            t = mm(bank(k)[:, 16 * p:16 * p + 16], one[0:1, :], rbr, False, True)
        t = cp("dve", lg, bank(k, 256).rearrange("p (b e) -> p b e", b=NP), t)
        free[k] = t
        t = red(small[:, 0:NP], lg, ALU.max, t)
        t = tt("dve", lg, lg, small[:, 0:NP].unsqueeze(2).broadcast_to([128, NP, 16]), ALU.subtract, t)
        t = act(lg, lg, ACT.Exp, t)
        t = red(small[:, 16:16 + NP], lg, ALU.add, t)
        t = put("dve", lambda g: g.reciprocal(small[:, 32:32 + NP], small[:, 16:16 + NP]), t)
        t = tt("dve", lg, lg, small[:, 32:32 + NP].unsqueeze(2).broadcast_to([128, NP, 16]), ALU.mult, t)
        t_s = rank_sel(lg, NP, 16, 4, tri, sel, t, g1, g2)
        t_ct = []
        for g4 in range(4):
            k, w = take()
            for q in range(4):
                t = tr(bank(k)[0:16, 128 * q:128 * q + 128], sel[:, 4 * g4 + q, :], idf[:, :], w, t_s, sig=(q == 3))
            free[k] = cp("act", selT[:, 512 * g4:512 * g4 + 512], bank(k)[0:16, :], t)
            t_ct += free[k]
        hid = [big[:, 16384:18432], big[:, 18432:20480]]
        rel = [big[:, 8192 + 448 * i:8192 + 448 * i + 448] for i in range(4)]
        zs = [zero("pool", h) for h in hid]
        use, r_use = [[], []], [[] for _ in range(4)]
        for c in range(4):
            u = c % 2
            hv = hid[u].rearrange("p (m n) -> p m n", m=4)
            t_h = []
            for m in range(4):
                k1, w = take()
                t1 = mm(bank(k1, 448), f1[:, m, :], tok8(xT, c), True, True, w)
                k2, w = take()
                t2 = mm(bank(k2, 448), spread[:, m, :], tok8(selT, c), True, True, w, t_ct)
                free[k1] = act(rel[m], bank(k1, 448), ACT.Relu, t1, r_use[m], bias=fb[:, m:m + 1])
                free[k2] = tt("dve", hv[:, m, :].rearrange("p (b q) -> p b q", q=64)[:, :, 0:NQ], q8(k2),
                              rel[m].rearrange("p (b q) -> p b q", q=NQ), ALU.mult, t2, free[k1], use[u], zs[u])
                r_use[m] = free[k2]
                t_h += free[k2]
            for q in range(4):
                p = 4 * c + q
                k, w = take()
                mm(bank(k, 128), one[0:1, :], crow[:, :], True, False, w, sig=False)
                for m in range(4):
                    t = mm(bank(k, 128), hv[:, m, 128 * q:128 * q + 128], f2[:, m, :], False, m == 3, t_h)
                use[u] = t
                free[k] = tt("dve", x[:, p, :], x[:, p, :], bank(k, 128), ALU.add, t)
        ov = out.rearrange("(p r) q d -> r q p d", r=2)
        t = P.all_done()
        for r in range(2):
            t_out = P.dma(s_out, ov[r], x[64 * r:64 * r + NQ, :, :], t)
        ends = t_out + stored

        block = ctx.enter_context(nc.Block())

        @block.sync
        def _(eng):
            P.run("sp", eng)
            for s, v in ends:
                eng.wait_ge(s, v)

        @block.tensor
        def _(eng):
            P.run("pe", eng)

        @block.vector
        def _(eng):
            P.run("dve", eng)

        @block.scalar
        def _(eng):
            P.run("act", eng)

        @block.gpsimd
        def _(eng):
            P.run("pool", eng)


def layout(i):
    import numpy as np

    f = {}
    f["x"] = i["x"]
    c = i["ctx_512"].reshape(B, KP, KT, C)
    f["ctxN"] = c.reshape(B, KP, KT * C)
    f["ctxT"] = c.transpose(0, 3, 2, 1).reshape(B, C, M)
    g = np.arange(128)
    f["ident"] = np.eye(128, dtype=np.float32)

    def cols(w, d):
        return w.reshape(w.shape[0], H, d).transpose(2, 1, 0)

    def rows(w, d):
        return w.reshape(H, d, w.shape[1]).transpose(1, 0, 2)

    f["L0q"], f["L0k"], f["L0v"] = (cols(i[f"L0_xattn_W{n}"], 64) for n in "qkv")
    f["L0o"] = rows(i["L0_xattn_Wo"], 64)
    f["L0bo"] = i["L0_xattn_bo"].reshape(1, 128)
    f["Wgate"] = i["L0_ffn_Wgate"]
    f["bgate"] = i["L0_ffn_bgate"].reshape(1, E)
    w1, w2, w3 = (i[f"L0_ffn_W{n}"] for n in "123")

    def halves(w):
        return w.reshape(E, 2, 128, -1).transpose(0, 2, 1, 3).reshape(E, 128, -1)

    f["ew"] = np.concatenate([w1, w2, halves(i["L0_ffn_Wg"]), halves(i["L0_ffn_Wl"]),
                              np.zeros((E, 128, 512), np.float32)], axis=2)
    f["ew3"] = halves(w3)
    f["ebias"] = np.stack([i[f"L0_ffn_{n}"].reshape(E, 2, 128) for n in ("b1", "b2", "bg", "bl")], 1) \
        .transpose(3, 0, 1, 2).reshape(128, E, 8)
    f["b3"] = i["L0_ffn_b3"]
    for n in (8, 16):
        f[f"tri{n}"] = np.ascontiguousarray(np.broadcast_to(np.tril(np.ones((n, n), np.float32), -1), (128, n, n)))
    f["L1q"] = rows(i["L1_xattn_Wq"], 8)
    f["L1k"] = rows(i["L1_xattn_Wkv"][:128], 8)
    f["L1v"] = rows(i["L1_xattn_Wkv"][128:], 8)
    f["L1o"] = rows(i["L1_xattn_Wo"].T, 8)
    f["rhsT"] = i["L1_ffn_rhs"].T
    f["L2q"], f["L2k"], f["L2v"] = (cols(i[f"L2_xattn_W{n}"], 8) for n in "qkv")
    f["L2o"] = rows(i["L2_xattn_Wo"], 8)
    f["L2b"] = np.stack([i["L2_xattn_bq"].reshape(H, 8).T, i["L2_xattn_bv"].reshape(H, 8).T], 1)
    f["L2bo"] = i["L2_xattn_bo"].reshape(1, 128)
    ang = 2 * np.pi * (np.outer(g, g) % 128) / 128
    f["dft"] = np.stack([np.cos(ang), np.sin(ang), -np.sin(ang)], 1).astype(np.float32)
    f["wfreq"] = np.stack([i["L2_ffn_w_freq_real"], i["L2_ffn_w_freq_imag"]], 1)
    f["L2bias"] = i["L2_ffn_bias"].reshape(1, 128)
    for n in ("a1", "a2"):
        for w in "qkv":
            f[f"{n}{w}"] = i[f"L3_xattn_{n}_w{w}"].transpose(2, 0, 1)
        f[f"{n}o"] = rows(i[f"L3_xattn_{n}_li1_w"], 32)
        f[f"{n}b1"] = i[f"L3_xattn_{n}_li1_b"].reshape(1, 128)
        f[f"{n}b3"] = i[f"L3_xattn_{n}_li3_b"].reshape(1, 128)
        f[f"{n}l2"] = i[f"L3_xattn_{n}_li2_w"].reshape(128, 4, 128)
        f[f"{n}l3"] = i[f"L3_xattn_{n}_li3_w"].reshape(4, 128, 128).transpose(1, 0, 2)
    p = "L3_xattn_"

    def li2b(n):
        return list(i[f"{p}{n}_li2_b"].reshape(4, 128))

    zero = np.zeros(128, np.float32)
    v = [i[p + n] for n in ("a1_lnx_g", "a1_lnx_b", "a1_lny_g", "a1_lny_b", "a1_ln3_g", "a1_ln3_b")] + li2b("a1")
    v += [i[p + n] for n in ("a2_lnx_g", "a2_lnx_b", "a2_ln3_g", "a2_ln3_b")] + li2b("a2")
    f["L3vec"] = np.stack(v + [zero] * (32 - len(v)), 1)
    f["L3bc"] = np.ascontiguousarray(np.broadcast_to(np.stack(
        [i[p + n] for n in ("ln1_g", "ln1_b", "a1_lny_g", "a1_lny_b", "ln2_g", "ln2_b")]), (128, 6, 128)))
    f["a2lyg"], f["a2lyb"] = (np.ascontiguousarray(np.broadcast_to(i[p + n], (128, C))) for n in ("a2_lny_g", "a2_lny_b"))
    r = np.arange(HQ).reshape(NJ, 128).T % NQ
    f["mask"] = (np.arange(NQ)[None, None, :] > r[:, :, None]).astype(np.float32)
    f["routerT"] = i["L3_ffn_router_w"].T
    f["routerb"] = i["L3_ffn_router_b"].reshape(1, 16)
    f["w1T"] = i["L3_ffn_w1"].T.reshape(128, 4, 128)
    f["w2T"] = i["L3_ffn_w2"].T.reshape(4, 128, 128).transpose(1, 0, 2)
    f["f1b"] = i["L3_ffn_b1"].reshape(4, 128).T
    f["f2b"] = i["L3_ffn_b2"].reshape(1, 128)
    f["spread"] = (np.arange(16)[:, None] == np.arange(512)[None, :] // 32).astype(np.float32).reshape(16, 4, 128)
    return {n: np.ascontiguousarray(w) for n, w in f.items()}


def kernel(**inputs):
    import numpy as np
    import concourse.bacc as bacc
    from concourse import mybir as mb
    from concourse.bass_utils import run_bass_kernel_spmd

    nc = bacc.Bacc("TRN2", target_bir_lowering=False, num_devices=1)
    host = layout({n: np.asarray(v) for n, v in inputs.items()})
    arrays = {f"in_{n}": v for n, v in host.items()}
    aps = {n: nc.dram_tensor(f"in_{n}", v.shape, mb.dt.from_np(v.dtype), kind="ExternalInput").ap()
           for n, v in host.items()}
    out = nc.dram_tensor("out_x", (B, NQ, D), F32, kind="ExternalOutput").ap()
    build(nc, aps, out)
    r = run_bass_kernel_spmd(nc, [arrays], core_ids=[0])
    return r.results[0]["out_x"]
```

```python
from contextlib import ExitStack

import concourse.bass as bass
from concourse import mybir

F32 = mybir.dt.float32
BF16 = mybir.dt.bfloat16
ALU = mybir.AluOpType
ACT = mybir.ActivationFunctionType
AX = mybir.AxisListType

B, NQ, D = 32, 56, 128
NP = B // 2
M, C = 1500, 64
KT, KP = 12, 125
H = 16
HQ = H * NQ
NJ = HQ // 128
HB = 16
EPS = 1e-5
E, F = 8, 256
RND = 12582912.0


class Prog:

    def __init__(self, new_sem):
        self.new_sem = new_sem
        self.q = {e: [] for e in ("pe", "act", "dve", "pool", "sp")}
        self.pending = {e: [] for e in self.q}
        self.seen = {e: {} for e in self.q}
        self.dma_count = {}
        self.stores = []
        self.era = 0
        self.start_era("in")

    def start_era(self, name):
        self.sem = {e: self.new_sem(f"{name}_{e}") for e in ("pe", "act", "dve", "pool")}
        self.count = {e: 0 for e in self.sem}

    def put(self, e, fn, *waits, sig=True):
        need = []
        if e == "pool" and self.count[e]:
            waits += ([(self.sem[e], self.count[e])],)
        for w in self.pending[e] + list(waits):
            for s, v in (w if isinstance(w, list) else [w]):
                if self.seen[e].get(s.name, 0) < v:
                    self.seen[e][s.name] = v
                    need.append((s, v))
        self.pending[e] = []
        if not sig:
            self.q[e].append((need, fn, None, 0))
            return []
        self.count[e] += 1
        self.q[e].append((need, fn, self.sem[e], 1))
        return [(self.sem[e], self.count[e])]

    def dma(self, sem, out, in_, *waits, e="sp"):
        need = []
        for w in self.pending[e] + list(waits):
            for s, v in w:
                if self.seen[e].get(s.name, 0) < v:
                    self.seen[e][s.name] = v
                    need.append((s, v))
        self.pending[e] = []
        self.dma_count[sem.name] = self.dma_count.get(sem.name, 0) + 16
        self.q[e].append((need, lambda g: g.dma_start(out, in_), sem, 16))
        return [(sem, self.dma_count[sem.name])]

    def all_done(self):
        return [(self.sem[e], self.count[e]) for e in self.sem if self.count[e]]

    def fence(self):
        done = self.all_done()
        for e in self.pending:
            self.pending[e] = self.pending[e] + [done]

    def run(self, e, eng):
        for need, fn, s, n in self.q[e]:
            for w, v in need:
                eng.wait_ge(w, v)
            ins = fn(eng)
            if s is not None:
                ins.then_inc(s, n)


def build(nc, a, out):
    with ExitStack() as ctx:
        def sb(name, shape, dt=F32):
            return ctx.enter_context(nc.sbuf_tensor(name, shape, dt))

        def sem(name):
            return ctx.enter_context(nc.semaphore(name))

        P = Prog(sem)
        put = P.put

        def mm(o, l, r, start, stop, *w, sig=True):
            return put("pe", lambda g: g.matmul(o, l, r, start=start, stop=stop, skip_group_check=True), *w, sig=sig)

        def tr(o, i, idn, *w, sig=True):
            return put("pe", lambda g: g.transpose(o, i, idn), *w, sig=sig)

        def act(o, i, f, *w, bias=0.0, scale=1.0):
            return put("act", lambda g: g.activation(o, i, f, bias=bias, scale=scale), *w)

        def tt(e, o, x, y, op, *w):
            return put(e, lambda g: g.tensor_tensor(o, x, y, op), *w)

        def ts(o, x, s1, s2, op0, op1, *w, e="dve"):
            if s2 is None:
                return put(e, lambda g: g.tensor_scalar(o, x, s1, None, op0), *w)
            return put(e, lambda g: g.tensor_scalar(o, x, s1, s2, op0, op1), *w)

        def stt(o, x, s, y, op0, op1, *w):
            return put("dve", lambda g: g.scalar_tensor_tensor(out=o, in0=x, scalar=s, in1=y, op0=op0, op1=op1), *w)

        def red(o, x, op, *w, negate=False, mag=False):
            return put("dve", lambda g: g.tensor_reduce(o, x, AX.X, op, negate=negate, apply_absolute_value=mag), *w)

        def cp(e, o, x, *w):
            if e == "act":
                return act(o, x, ACT.Copy, *w)
            return put(e, lambda g: g.tensor_copy(o, x), *w)

        def zero(e, o, v=0.0):
            return put(e, lambda g: g.memset(o, v))

        ps = ctx.enter_context(nc.psum_tensor("ps", [128, 4096], F32))

        def bank(k, n=512):
            return ps[:, 512 * k:512 * k + n]

        x = sb("x", [128, NP, D])
        xn = sb("xn", [128, NP, D])
        xT = sb("xT", [128, NP * 128])
        idf = sb("idf", [128, 128])
        idb = sb("idb", [128, 128], BF16)
        one = sb("one", [128, 128])
        crow = sb("crow", [1, 128])
        rowb = sb("rowb", [1, 512])
        st = sb("st", [128, NP, 6])
        mv = sb("mv", [128, NP, 2])
        ve = sb("ve", [128, NP])
        rs = sb("rs", [128, NP])
        mhalf = sb("mhalf", [128, NP])
        small = sb("small", [128, 64])
        big = sb("big", [128, 21504])
        wa = sb("wa", [128, H * 128])
        wb = sb("wb", [128, H * 128])
        wst = sb("wst", [128, 6144])
        wbh = wb[:, 0:1024].bitcast(BF16)
        wbl = wb[:, 1024:2048].bitcast(BF16)
        wbhv, wblv = (w.rearrange("p (h n) -> p h n", h=H) for w in (wbh, wbl))
        Qh = big[:, 0:7168].bitcast(BF16).rearrange("p (b n) -> p b n", b=HB)
        Ql = big[:, 7168:14336].bitcast(BF16).rearrange("p (b n) -> p b n", b=HB)
        O = big[:, 14336:21504].bitcast(BF16).rearrange("p (b j c) -> p b j c", b=HB, j=NJ)
        cTs = sb("cTs", [128, 2 * M])
        cT = [cTs[:, M * i:M * i + M] for i in range(2)]
        cx = sb("cx", [128, 7608])
        cs = [cx[:, 750 * i:750 * i + 750].bitcast(BF16) for i in range(3)]
        chx = [cx[0:67, 2250 + 750 * i:3000 + 750 * i].bitcast(BF16) for i in range(2)]
        cn = [cx[0:KP, 3750 + 768 * i:4518 + 768 * i].rearrange("p (t c) -> p t c", t=KT) for i in range(2)]
        cnb = [cx[0:KP, 5286 + 774 * i:6060 + 774 * i].bitcast(BF16).rearrange("p (t c) -> p t c", t=KT) for i in range(3)]
        pf = [wst[:, HQ * i:HQ * i + HQ] for i in range(3)]
        pl = [wst[:, 2688 + 448 * i:3136 + 448 * i].bitcast(BF16) for i in range(3)]
        raw = [wst[:, 4032 + 903 * i:4935 + 903 * i].rearrange("p (j c) -> p j c", j=NJ) for i in range(2)]
        mx = [wst[:, 5838 + 21 * i:5859 + 21 * i].rearrange("p (j c) -> p j c", j=NJ) for i in range(2)]
        nm = [wst[:, 5880 + 21 * i:5901 + 21 * i].rearrange("p (c j) -> p c j", c=3) for i in range(2)]
        m3 = [sb(f"m3{i}", [128, NJ, 3], BF16) for i in range(2)]
        rden = [sb(f"rden{i}", [128, NJ]) for i in range(2)]

        s_in = sem("s_in")
        s_w = sem("s_w")
        s_e = [sem("s_e0"), sem("s_e1")]
        s_cT = [sem("s_cT0"), sem("s_cT1")]
        s_cn = [sem("s_cn0"), sem("s_cn1")]
        s_sT = [sem("s_sT0"), sem("s_sT1")]
        s_sn = [sem("s_sn0"), sem("s_sn1"), sem("s_sn2")]
        s_bc = sem("s_bc")
        s_out = sem("s_out")

        yT = nc.dram_tensor("ynT", [B, C, M], F32).ap()
        yN = nc.dram_tensor("ynN", [B, KP, KT * C], F32).ap()

        free = [[] for _ in range(8)]
        turn = [0]

        def take():
            k = turn[0] % 8
            turn[0] += 1
            return k, free[k]

        def evac_e(n):
            return "act" if n % 2 else "dve"

        zx = zero("dve", x[:, :, :])
        zm = zero("pool", mhalf[:, :], -0.5)
        zo = zero("pool", one[:, :], 1.0)
        t_in = []
        xv = a["x"].rearrange("(p r) q d -> r q p d", r=2)
        for r in range(2):
            t_in = P.dma(s_in, x[64 * r:64 * r + NQ, :, :], xv[r], zx)
        t_in = P.dma(s_in, idf[:, :], a["ident"])
        cp("pool", idb[:, :], idf[:, :], t_in)
        P.fence()
        for e in ("pe", "dve", "act", "pool"):
            P.pending[e].append(t_in)

        def layernorm(src, dst):
            t = []
            for p in range(NP):
                t = put("dve", lambda g, p=p: g.bn_stats(st[:, p, :], src[:, p, :]))
            for p in range(NP):
                t2 = put("dve", lambda g, p=p: g.bn_aggr(mv[:, p, :], st[:, p, :]), t)
            t = ts(ve[:, :], mv[:, :, 1], EPS, None, ALU.add, None, t2)
            t = tt("pool", rs[:, :], ve[:, :], mhalf[:, :], ALU.pow, t)
            return [ts(dst[:, p, :], src[:, p, :], mv[:, p, 0:1], rs[:, p:p + 1], ALU.subtract, ALU.mult, t)
                    for p in range(NP)]

        def transpose_all(src, ready, *dsts):
            done = []
            for g4 in range(4):
                k, w = take()
                for q in range(4):
                    t = tr(bank(k)[:, 128 * q:128 * q + 128], src[:, 4 * g4 + q, :], idf[:, :],
                           w, ready[4 * g4 + q], sig=(q == 3))
                for dst, g, b in dsts:
                    o = dst[:, 512 * g4:512 * g4 + 512]
                    if g is None:
                        r = cp(evac_e(g4), o, bank(k), t)
                    else:
                        r = ts(o, bank(k), g, b, ALU.mult, ALU.add, t)
                free[k] = r
                done += free[k]
            return done

        def tok8(t, c):
            return t[:, 512 * c:512 * c + 512].rearrange("p (b q) -> p b q", q=64)[:, :, 0:NQ]

        def q8(k):
            return bank(k, 448).rearrange("p (b q) -> p b q", q=NQ)

        def fold(n, nd, wq, wk, wv, wo, dup, ready):
            done = []
            per = 512 // n
            wav = wa[:, :].rearrange("p (h r c) -> p h r c", h=H, r=128 // n)
            for h0 in range(0, H, per):
                k, w = take()
                for h in range(h0, h0 + per):
                    t = mm(bank(k)[:, n * (h - h0):n * (h - h0) + n], wq[0:nd, h, :], wk[0:nd, h, :], True, True,
                           w, ready, sig=(h == h0 + per - 1))
                src = bank(k).rearrange("p (h c) -> p h c", c=n)
                r = []
                for d in range(128 // n if dup else 1):
                    r = cp(evac_e(h0 // per), wav[:, h0:h0 + per, d, :], src, t)
                free[k] = r
                done += r
            for h0 in range(0, H, 4):
                k, w = take()
                for h in range(h0, h0 + 4):
                    t = mm(bank(k)[0:n, 128 * (h - h0):128 * (h - h0) + 128], wv[0:nd, h, :], wo[0:nd, h, :], True, True,
                           w, ready, sig=(h == h0 + 3))
                cols = slice(128 * h0, 128 * h0 + 512)
                th = tl = []
                for r in range(128 // n):
                    th = act(wbh[n * r:n * r + n, cols], bank(k)[0:n, :], ACT.Copy, t)
                for r in range(128 // n):
                    tl = tt("dve", wbl[n * r:n * r + n, cols], bank(k)[0:n, :], wbh[0:n, cols], ALU.subtract, t, th)
                free[k] = th + tl
                done += free[k]
            return done

        def load_w(names, ready=[]):
            views, at, t = [], 0, []
            for name in names:
                d, h, n = a[name].shape
                v = wst[0:d, at:at + h * n].rearrange("d (h n) -> d h n", h=h)
                at += h * n
                t = P.dma(s_w, v, a[name], ready)
                views.append(v)
            return views, t

        def rows_in(names):
            at, t, o = 0, [], []
            for name in names:
                n = a[name].shape[1]
                t = P.dma(s_w, rowb[0:1, at:at + n], a[name])
                o.append(rowb[0:1, at:at + n])
                at += n
            return o, t

        wav = wa[:, :].rearrange("p (h n) -> p h n", h=H)

        def cross(scale, srcN, srcT, qsrc, add_to, bias=None):
            for k in range(3):
                if k < 2:
                    zero("pool", chx[k][64:67, :], 1.0)
                zero("pool", cnb[k][:, :, C:C + 1], 1.0)
            xnf = xn[:, :, :].rearrange("c p d -> c (p d)")
            ob = [xnf[:, 1024 * i:1024 * i + 1024].bitcast(BF16).rearrange("c (h q) -> c h q", h=H) for i in range(2)]
            t_ob = zero("pool", xnf)
            k, w = take()
            t = mm(bank(k, 128), one[0:1, :], crow[0:1, :], True, True, w)
            free[k] = tt("dve", add_to[:, :, :], add_to[:, :, :], bank(k, 128).unsqueeze(1).broadcast_to([128, NP, D]), ALU.add, t)

            def project_mm(c, h, k, w):
                return mm(bank(k, 448), wav[:, h, :], tok8(qsrc, c), True, True, w)

            def project_split(c, h, k, t, w):
                at = 8 * (c % 2)
                o = slice(at, at + 8), slice(NQ * h, NQ * h + NQ)
                bq = 0.0 if bias is None else bias[:, h:h + 1]
                t1 = act(Qh[:, o[0], o[1]], q8(k), ACT.Identity, t, w, bias=bq)
                bl = 0.0 if bias is None else bias[0:64, h:h + 1]
                t2 = stt(Ql[0:64, o[0], o[1]], q8(k)[0:64], bl, Qh[0:64, o[0], o[1]],
                         ALU.add, ALU.subtract, t, t1, w)
                return t1 + t2

            t_proj = {}
            for h in range(H):
                k, w = take()
                t_proj[0] = free[k] = project_split(0, h, k, project_mm(0, h, k, w), [])
            P.fence()
            for k in range(8):
                free[k] = []

            cT_free, cn_free = [[], []], [[], []]
            cs_use, chx_use, cnb_use = [[], [], []], [[], []], [[], [], []]
            t_cT, t_cn, t_cs, t_cl, t_chx, t_cnb, t_cnl = {}, {}, {}, {}, {}, {}, {}
            s1_free, s2_free = [[], []], [[], [], []]
            n1, n2 = [0], [0]
            t_max, t_m3, t_rows, t_neg = {}, {}, {}, {}
            pf_free = [[], [], []]
            t_exp, t_pl, t_pv, t_last, t_fin, t_gone = {}, {}, {}, {}, {}, {}
            pv_free = []
            raw_free = [[], []]

            def load(k):
                s = k % 2
                P.dma(s_cT[s], cT[s][0:64, :], srcT[k], cT_free[s])
                t_cT[k] = P.dma(s_cT[s], cT[s][64:128, :], srcT[k], cT_free[s])
                t_cn[k] = P.dma(s_cn[s], cn[s].rearrange("p t c -> p (t c)"), srcN[k], cn_free[s])

            def cast_a(k):
                s, u = k % 2, k % 3
                t_cs[k] = act(cs[u], cT[s], ACT.Copy, t_cT[k], cs_use[u])
                t_cl[k] = tt("pool", cs[u][64:128, :], cT[s][64:128, :], cs[u][64:128, :], ALU.subtract, t_cs[k])

            def cast_b(k):
                s = k % 2
                t_chx[k] = act(chx[s][0:64, :], cT[s][0:64, :], ACT.Copy, t_cT[k], chx_use[s])
                cT_free[s] = t_chx[k] + t_cl[k]

            def cast_c(k):
                s, u = k % 2, k % 3
                t_cnb[k] = act(cnb[u][:, :, 0:C], cn[s], ACT.Copy, t_cn[k], cnb_use[u])
                t_cnl[k] = tt("pool", cnb[u][:, :, C + 1:], cn[s], cnb[u][:, :, 0:C], ALU.subtract, t_cnb[k])
                cn_free[s] = t_cnl[k]

            def chunk(k, n):
                j, c = n // 3, n % 3
                s = n1[0] % 2
                n1[0] += 1
                t = mm(bank(s, 500), Qh[:, k % HB, 128 * j:128 * j + 128], cs[k % 3][:, 500 * c:500 * c + 500], True, True,
                       s1_free[s], t_cl[k], t_proj[k // 8])
                s1_free[s] = t_max[k] = red(mx[k % 2][:, j, c:c + 1], bank(s, 500), ALU.max, t)

            def maxima(k):
                s = k % 2
                q = nm[s]
                t = red(q[:, 0, :], mx[s], ALU.max, t_max[k], t_m3.get(k - 2, []), negate=True)
                for n in range(3):
                    t = put("pool", lambda g, n=n: g.tensor_copy(m3[s][:, :, n], q[:, n, :]), t, t_rows.get(k - 2, []))
                    if n < 2:
                        t = tt("pool", q[:, n + 1, :], q[:, n, :], m3[s][:, :, n], ALU.subtract, t)
                t_m3[k] = t

            def rows(k):
                done = []
                for j0, j1 in ((0, 4), (4, NJ)):
                    s = n2[0] % 3
                    n2[0] += 1
                    for j in range(j0, j1):
                        t = mm(bank(2 + s)[64:67, 128 * (j - j0):128 * (j - j0) + 128], m3[k % 2][:, j, :], idb[:, :],
                               True, True, s2_free[s], t_m3[k], sig=(j == j1 - 1))
                    s2_free[s] = cp("act", Ql[64:67, k % HB, 128 * j0:128 * j1], bank(2 + s)[64:67, 0:128 * (j1 - j0)],
                                    t, t_last.get(k - HB, []))
                    done += s2_free[s]
                    t_rows[k] = t
                t_neg[k] = done

            def scores(T):
                k, t = divmod(T, KT)
                u, r = k % 3, T % 3
                done = []
                for hf in range(2):
                    s = n2[0] % 3
                    n2[0] += 1
                    cols = slice(448 * hf, 448 * hf + 448)
                    keys = slice(KP * t, KP * t + KP)
                    mm(bank(2 + s, 448)[0:KP], cs[u][:, keys], Qh[:, k % HB, cols], True, False,
                       s2_free[s], t_cl[k], t_proj[k // 8], sig=False)
                    w = mm(bank(2 + s, 448)[0:KP], chx[k % 2][:, keys], Ql[0:67, k % HB, cols], False, True,
                           t_neg[k], t_chx[k])
                    if t == KT - 1:
                        cs_use[u] = chx_use[k % 2] = t_last[k] = w
                    s2_free[s] = act(pf[r][0:KP, cols], bank(2 + s, 448)[0:KP], ACT.Exp, w, pf_free[r], scale=scale)
                    done += s2_free[s]
                t_exp[T] = done

            def rest(T):
                r = T % 3
                t_pl[T] = tt("dve", pl[r][0:KP, :], pf[r][0:KP, :], pf[r][0:KP, :].bitcast(BF16)[:, 1::2],
                             ALU.subtract, t_exp[T], pf_free[r])

            def pv(T):
                k, t = divmod(T, KT)
                u, r = k % 3, T % 3
                ph = pf[r][0:KP, :].bitcast(BF16)[:, 1::2]
                first = t == 0
                for j in range(NJ):
                    cols = slice(128 * j, 128 * j + 128)
                    at = 2560 + 129 * j
                    n = min(129, 3072 - at) if at < 3072 else 129
                    mm(ps[:, at:at + n], ph[:, cols], cnb[u][:, t, 0:n], first and j == 0, False,
                       pv_free, t_pl[T], t_cnl[k], sig=False)
                    if n < 129:
                        mm(ps[:, at + n:at + 129], ph[:, cols], cnb[u][:, t, n:129], first, False, sig=False)
                    w = mm(ps[:, at:at + 65], pl[r][0:KP, cols], cnb[u][:, t, 0:65], False, t == KT - 1,
                           sig=(j == NJ - 1))
                pf_free[r] = w
                t_pv[T] = w
                if t == KT - 1:
                    cnb_use[u] = w

            def finish(k):
                s = k % 2
                done = cp("act", raw[s].rearrange("p j c -> p (j c)"), ps[:, 2560:2560 + 129 * NJ],
                          t_pv[KT * k + KT - 1], raw_free[s])
                pv_free[:] = done
                t = put("dve", lambda g: g.reciprocal(rden[s][:, :], raw[s][:, :, C]), done, raw_free[s])
                v = raw[s][:, :, 0:C]
                t1 = tt("pool", v, v, raw[s][:, :, C + 1:], ALU.add, done)
                t1 = tt("pool", v, v, rden[s][:, :].unsqueeze(2).broadcast_to([128, NJ, C]), ALU.mult, t, t1)
                t2 = cp("pool", O[:, k % HB, :, 0:C], v, t1, t_gone.get(k - HB, []))
                t2 = tt("pool", O[:, k % HB, :, C:], v, O[:, k % HB, :, 0:C], ALU.subtract, t2)
                raw_free[s] = t_fin[k] = t2

            def between():
                f7 = []
                ob_use = [[], []]
                for c in range(5):
                    while 8 * c - 1 not in t_last and c > 0:
                        yield
                    for i in range(4):
                        if c < 3:
                            for h in range((0, 6, 12, 16)[i], (6, 12, 16, 16)[i]):
                                t = project_mm(c + 1, h, 7, f7)
                                yield
                                f7 = project_split(c + 1, h, 7, t, t_last.get(8 * c - 1, []))
                                t_proj[c + 1] = f7
                                yield
                        p = 4 * c - 1 + i
                        if not 0 <= p < NP:
                            continue
                        t_o = []
                        for r in range(2):
                            k = 2 * p + r
                            while k not in t_fin or now[0] < KT * k + KT + 9:
                                yield
                            v = bank(7).bitcast(BF16)
                            for j in range(NJ):
                                t = tr(v[:, 128 * j:128 * j + 128], O[:, k % HB, j, :], idb[:, :], f7, t_fin[k], sig=(j == NJ - 1))
                            t_gone[k] = t
                            yield
                            f7 = cp("act", ob[p % 2][:, :, 64 * r:64 * r + NQ],
                                    v[:, 0:HQ].rearrange("c (h q) -> c h q", h=H), t, t_ob, ob_use[p % 2])
                            t_o += f7
                            yield
                        for h in range(H):
                            mm(bank(7, 128), ob[p % 2][:, h, :], wbhv[:, h, :], h == 0, False, f7, t_o, sig=False)
                            t = mm(bank(7, 128), ob[p % 2][:, h, :], wblv[:, h, :], False, h == H - 1, sig=(h == H - 1))
                            if h == 7:
                                yield
                        ob_use[p % 2] = t
                        yield
                        f7 = tt("dve", add_to[:, p, :], add_to[:, p, :], bank(7, 128), ALU.add, t)
                        yield

            now = [0]
            bg = between()
            for T in range(-26, KT * B + 3):
                for k in range(B):
                    if T == KT * k - 26:
                        load(k)
                    if T == KT * k - 23:
                        cast_a(k)
                    if T == KT * k - 10:
                        cast_b(k)
                    if T == KT * k - 19:
                        cast_c(k)
                    if T == KT * k - 3:
                        maxima(k)
                    if T == KT * k - 2:
                        rows(k)
                    if T == KT * k + KT + 2:
                        finish(k)
                turns = [(k, n) for k in range(B) for n in range(21) if T == KT * k - 16 + n * KT // 21]
                if turns:
                    chunk(*turns[0])
                if 0 <= T < KT * B:
                    scores(T)
                if 0 <= T - 1 < KT * B:
                    rest(T - 1)
                for k, n in turns[1:]:
                    chunk(k, n)
                if 0 <= T - 2 < KT * B:
                    pv(T - 2)
                now[0] = T
                if T >= 0:
                    next(bg, None)
            for _ in bg:
                now[0] += 1
            P.fence()
            for k in range(8):
                free[k] = []

        def layer(name):
            P.fence()
            P.start_era(name)
            for k in range(8):
                free[k] = []

        ctxN, ctxT = a["ctxN"], a["ctxT"]
        (wq, wk, wv), tw = load_w(["L0q", "L0k", "L0v"])
        wo0 = big[0:64, 0:2048].rearrange("d (h n) -> d h n", h=H)
        P.dma(s_w, wo0, a["L0o"])
        tw = P.dma(s_w, crow[:, :], a["L0bo"])
        n = layernorm(x, xn)
        transpose_all(xn, n, (xT, None, None))
        fold(64, 64, wq, wk, wv, wo0, True, tw)
        layer("L0a")
        cross(64 ** -0.5, ctxN, ctxT, xT, x)

        gw = wst[:, 4096:4104]
        P.dma(s_w, gw, a["Wgate"])
        P.dma(s_w, crow[0:1, 0:E], a["bgate"])
        tri = wst[:, 4224:4224 + 64].rearrange("p (i j) -> p i j", i=E)
        P.dma(s_w, tri, a["tri8"])
        b3 = wst[0:E, 4352:4480]
        P.dma(s_w, b3, a["b3"])
        ebias = wst[:, 4480:4480 + 64].rearrange("p (e k) -> p e k", e=E)
        tw = P.dma(s_w, ebias, a["ebias"])
        ew = [wst[:, 0:2048], wst[:, 2048:4096]]
        ew3 = [wst[:, 4608:4864], wst[:, 4864:5120]]

        def load_e(e, *w):
            s = e % 2
            P.dma(s_e[s], ew[s], a["ew"][e], *w)
            return P.dma(s_e[s], ew3[s], a["ew3"][e], *w)

        te = {e: load_e(e) for e in range(2)}
        n = layernorm(x, xn)
        t_x = transpose_all(xn, n, (xT, None, None))

        def rank_sel(val, nb, ne, top, tri_, sel, ready, g1, g2):
            vi = val.unsqueeze(3).broadcast_to([128, nb, ne, ne])
            vj = val.unsqueeze(2).broadcast_to([128, nb, ne, ne])
            t = []
            for p in range(nb):
                t1 = tt("dve", g1[:, p], vj[:, p], vi[:, p], ALU.is_ge, ready)
                t2 = tt("dve", g2[:, p], vj[:, p], vi[:, p], ALU.is_gt, ready)
                t1 = tt("dve", g1[:, p], g1[:, p], tri_, ALU.mult, t1)
                t2 = tt("dve", g1[:, p], g1[:, p], g2[:, p], ALU.max, t1, t2)
                t = red(ve_big[:, p * ne:(p + 1) * ne], g1[:, p], ALU.add, t2)
            return ts(sel, ve_big[:, 0:nb * ne].rearrange("p (b e) -> p b e", b=nb), float(top), None, ALU.is_lt, None, t)

        ve_big = big[:, 12288:12544]
        g1 = big[:, 8192:9216].rearrange("p (b i j) -> p b i j", b=NP, i=E)
        g2 = big[:, 9216:10240].rearrange("p (b i j) -> p b i j", b=NP, i=E)
        lg = big[:, 12544:12672].rearrange("p (b e) -> p b e", b=NP)
        sel = big[:, 12672:12800].rearrange("p (b e) -> p b e", b=NP)
        comb = big[:, 12800:12928].rearrange("p (b e) -> p b e", b=NP)
        combT = big[0:E, 13000:13000 + 2048]
        k, w = take()
        for p in range(NP):
            mm(bank(k)[:, E * p:E * p + E], xT[:, 128 * p:128 * p + 128], gw, True, False, w, tw, t_x, sig=False)
            t = mm(bank(k)[:, E * p:E * p + E], one[0:1, :], crow[0:1, 0:E], False, True)
        t = cp("dve", lg, bank(k, 128).rearrange("p (b e) -> p b e", b=NP), t)
        free[k] = t
        t_s = rank_sel(lg, NP, E, 2, tri, sel, t, g1, g2)
        t1 = red(small[:, 0:NP], lg, ALU.max, t)
        t1 = tt("dve", lg, lg, small[:, 0:NP].unsqueeze(2).broadcast_to([128, NP, E]), ALU.subtract, t1, t_s)
        t1 = act(lg, lg, ACT.Exp, t1)
        t1 = tt("dve", comb, lg, sel, ALU.mult, t1, t_s)
        t2 = red(small[:, 16:16 + NP], comb, ALU.add, t1)
        t2 = put("dve", lambda g: g.reciprocal(small[:, 32:32 + NP], small[:, 16:16 + NP]), t2)
        t_c = tt("dve", comb, comb, small[:, 32:32 + NP].unsqueeze(2).broadcast_to([128, NP, E]), ALU.mult, t2)
        for g4 in range(4):
            k, w = take()
            for q in range(4):
                t = tr(bank(k)[0:E, 128 * q:128 * q + 128], comb[:, 4 * g4 + q, :], idf[:, :], w, t_c, sig=(q == 3))
            free[k] = cp("act", combT[:, 512 * g4:512 * g4 + 512], bank(k)[0:E, :], t)
        t_ct = free[k]
        t_acc = {}
        for p in range(NP):
            k, w = take()
            t = mm(bank(k, 128), combT[:, 128 * p:128 * p + 128], b3, True, True, w, t_ct)
            free[k] = t_acc[p] = tt("dve", x[:, p, :], x[:, p, :], bank(k, 128), ALU.add, t)
        z1 = [big[:, 0:896], big[:, 896:1792]]
        zz = [big[:, 1792:2688], big[:, 2688:3584]]
        sg = [big[:, 3584:4480], big[:, 4480:5376]]
        oo = [big[:, 5376:6400], big[:, 6400:7424]]
        t_z = [zero("pool", o) for o in oo]

        bcx = [wst[:, 5120:5184], wst[:, 5184:5248]]
        P.dma(s_bc, bcx[0], a["a2lyg"])
        t_bc = P.dma(s_bc, bcx[1], a["a2lyb"])
        at3 = [15360 + 1600 * i for i in range(3)]
        ns = [big[0:KP, o:o + 768].rearrange("p (t c) -> p t c", c=C) for o in at3]
        nsq = [big[0:KP, o + 768:o + 1536].rearrange("p (t c) -> p t c", c=C) for o in at3]
        nst = [big[0:KP, o + 1536:o + 1600].rearrange("p (k t) -> p k t", k=4)[:, :, 0:KT] for o in at3]
        nT = [cT[i][0:64] for i in range(2)]
        ncn_free, sn, sT, n_use = [[], []], [[], [], []], [[], []], [[], [], []]
        t_l, t_sq, t_n = {}, {}, {}

        def norm_load(b):
            s = b % 2
            t_l[b] = P.dma(s_cn[s], cn[s].rearrange("p t c -> p (t c)"), ctxN[b], ncn_free[s])

        def norm_a(b):
            s, u = b % 2, b % 3
            v, q = ns[u], nst[u]
            t = red(q[:, 0, :], cn[s], ALU.add, t_l[b], t_n.get(b - 3, []))
            t = ts(q[:, 1, :], q[:, 0, :], -1.0 / C, None, ALU.mult, None, t)
            t = tt("dve", v, cn[s], q[:, 1, :].unsqueeze(2).broadcast_to([KP, KT, C]), ALU.add, t, sn[u], n_use[u])
            ncn_free[s] = t
            t_sq[b] = act(nsq[u], v, ACT.Square, t)

        def norm_b(b):
            u = b % 3
            v, q = ns[u], nst[u]
            t = red(q[:, 2, :], nsq[u], ALU.add, t_sq[b])
            t = ts(q[:, 2, :], q[:, 2, :], 1.0 / C, EPS, ALU.mult, ALU.add, t)
            t = tt("pool", q[:, 3, :], q[:, 2, :], mhalf[0:KP, 0:KT], ALU.pow, t)
            t = tt("pool", v, v, q[:, 3, :].unsqueeze(2).broadcast_to([KP, KT, C]), ALU.mult, t)
            t = tt("pool", v, v, bcx[0][0:KP].unsqueeze(1).broadcast_to([KP, KT, C]), ALU.mult, t, t_bc)
            t_n[b] = tt("pool", v, v, bcx[1][0:KP].unsqueeze(1).broadcast_to([KP, KT, C]), ALU.add, t)

        def norm_c(b):
            s, u = b % 2, b % 3
            sn[u] = P.dma(s_sn[u], yN[b], ns[u].rearrange("p t c -> p (t c)"), t_n[b])
            done = []
            for g in range(3):
                k, w = take()
                for i in range(4):
                    t = tr(bank(k)[0:64, KP * i:KP * i + KP], ns[u][:, 4 * g + i, :], idf[0:KP, 0:KP], w, t_n[b], sig=(i == 3))
                free[k] = cp("act", nT[s][:, 500 * g:500 * g + 500], bank(k, 500)[0:64], t, sT[s])
                done += free[k]
            n_use[u] = t
            sT[s] = P.dma(s_sT[s], yT[b], nT[s], done)

        norm_load(0)
        z_use, o_use = [[], []], [[], []]
        t_zf, t_o = {}, {}

        def up(n):
            e, c = divmod(n, 4)
            s, u = e % 2, n % 2
            w1 = ew[s][:, 0:256]
            w2 = ew[s][:, 256:512]
            t_zf[n] = []
            for f in range(2):
                cols = slice(128 * f, 128 * f + 128)
                half = slice(448 * f, 448 * f + 448)
                k1, w = take()
                t1 = mm(bank(k1, 448), w1[:, cols], tok8(xT, c), True, True, w, te[e])
                k2, w = take()
                t2 = mm(bank(k2, 448), w2[:, cols], tok8(xT, c), True, True, w)
                free[k1] = act(z1[u][:, half], bank(k1, 448), ACT.Identity, t1, z_use[u], bias=ebias[:, e, f:f + 1])
                free[k2] = stt(zz[u][:, half], bank(k2, 448), ebias[:, e, 2 + f:3 + f], z1[u][:, half],
                               ALU.add, ALU.mult, t2, free[k1], z_use[u])
                t_zf[n].append(free[k2])

        def mid(n):
            e, c = divmod(n, 4)
            s, u = e % 2, n % 2
            wg = ew[s][:, 512:1024].rearrange("p (k n) -> p k n", k=2)
            wl = ew[s][:, 1024:1536].rearrange("p (k n) -> p k n", k=2)
            t_o[n] = []
            for f in range(2):
                cols = slice(128 * f, 128 * f + 128)
                half = slice(448 * f, 448 * f + 448)
                k1, w = take()
                for i in range(2):
                    t1 = mm(bank(k1, 448), wg[:, i, cols], zz[u][:, 448 * i:448 * i + 448], i == 0, i == 1,
                            w, t_zf[n][i], sig=(i == 1))
                k2, w = take()
                for i in range(2):
                    t2 = mm(bank(k2, 448), wl[:, i, cols], zz[u][:, 448 * i:448 * i + 448], i == 0, i == 1,
                            w, sig=(i == 1))
                ta = act(sg[u][:, half], bank(k1, 448), ACT.Sigmoid, t1, o_use[u], bias=ebias[:, e, 4 + f:5 + f])
                tb = stt(sg[u][:, half], bank(k1, 448), ebias[:, e, 4 + f:5 + f], sg[u][:, half], ALU.add, ALU.mult, ta)
                free[k1] = ta + tb
                ov = oo[u][:, 512 * f:512 * f + 512].rearrange("p (b q) -> p b q", q=64)[:, :, 0:NQ]
                free[k2] = stt(ov, q8(k2), ebias[:, e, 6 + f:7 + f], sg[u][:, half].rearrange("p (b q) -> p b q", q=NQ),
                               ALU.add, ALU.mult, t2, tb, o_use[u], t_z[u])
                t_o[n] += free[k2]
            z_use[u] = t2

        def down(n):
            e, c = divmod(n, 4)
            s, u = e % 2, n % 2
            w3 = ew3[s].rearrange("p (k n) -> p k n", k=2)
            k, w = take()
            r = []
            for q in range(4):
                for i in range(2):
                    t = mm(bank(k)[:, 128 * q:128 * q + 128], oo[u][:, 512 * i + 128 * q:512 * i + 128 * q + 128],
                           w3[:, i, :], i == 0, i == 1, w, t_o[n], sig=(q == 3 and i == 1))
            o_use[u] = t
            for q in range(4):
                p = 4 * c + q
                t_acc[p] = stt(x[:, p, :], bank(k)[:, 128 * q:128 * q + 128], comb[:, p, e:e + 1], x[:, p, :],
                               ALU.mult, ALU.add, o_use[u], t_acc[p])
                r += t_acc[p]
            free[k] = r
            if c == 3 and e + 2 < E:
                te[e + 2] = load_e(e + 2, o_use[u])

        for n in range(4 * E + 2):
            if n < 4 * E:
                up(n)
            if 1 <= n <= 4 * E:
                mid(n - 1)
            if n >= 2:
                down(n - 2)
            if n + 1 < B:
                norm_load(n + 1)
            if n < B:
                norm_a(n)
            if 1 <= n <= B:
                norm_b(n - 1)
            if 2 <= n <= B + 1:
                norm_c(n - 2)
        stored = sum(sn + sT, [])
        layer("L1a")

        (wq, wk, wv), tw = load_w(["L1q", "L1k", "L1v"])
        wo1 = big[0:8, 0:2048].rearrange("d (h n) -> d h n", h=H)
        tw = P.dma(s_w, wo1, a["L1o"])
        t0 = zero("pool", crow[:, :])
        n = layernorm(x, xn)
        transpose_all(xn, n, (xT, None, None))
        fold(64, 8, wq, wk, wv, wo1, True, tw)
        layer("L1b")
        cross(8 ** -0.5, ctxN, ctxT, xT, x)

        rT = wst[:, 0:128]
        tw = P.dma(s_w, rT, a["rhsT"])
        n = layernorm(x, xn)
        qf = big[:, 0:2048].rearrange("p (b d) -> p b d", b=NP)
        xq = big[:, 2048:3072].bitcast(BF16)
        rq = wst[:, 128:256]
        rqb = wst[:, 256:320].bitcast(BF16)
        dg = wst[:, 384:512]
        rsb = wst[:, 512:640]
        amax = small[:, 0:17]
        scl = small[:, 17:34]
        inv = small[:, 34:51]
        t1 = red(amax[:, 0:NP], xn[:, :, :], ALU.max, sum(n, []), mag=True)
        t2 = red(amax[:, 16:17], rT, ALU.max, tw, mag=True)
        t = ts(scl, amax, 1e-12, 1.0 / 127.0, ALU.max, ALU.mult, t1, t2)
        t_s = put("dve", lambda g: g.reciprocal(inv, scl), t)

        def quantize(o, i, s, *w):
            t = ts(o, i, s, RND, ALU.mult, ALU.add, *w)
            t = ts(o, o, -RND, 127.0, ALU.add, ALU.min, t)
            return ts(o, o, -127.0, None, ALU.max, None, t)

        n = [quantize(qf[:, p, :], xn[:, p, :], inv[:, p:p + 1], t_s) for p in range(NP)]
        t_x = transpose_all(qf, n, (xq, None, None))
        t = quantize(rq, rT, inv[:, 16:17], t_s, tw)
        k, w = take()
        t = tr(bank(k, 128), rq, idf[:, :], w, t)
        t_r = cp("act", rqb, bank(k, 128), t)
        free[k] = t_r
        t = ts(dg, idf[:, :], scl[:, 16:17], None, ALU.mult, None, t_s)
        k, w = take()
        t = mm(bank(k, 128), one[:, :], dg, True, True, w, t)
        t_b = cp("act", rsb, bank(k, 128), t)
        free[k] = t_b
        for p in range(NP):
            k, w = take()
            t = mm(bank(k, 128), xq[:, 128 * p:128 * p + 128], rqb, True, True, w, t_x, t_r)
            free[k] = stt(qf[:, p, :], bank(k, 128), scl[:, p:p + 1], rsb, ALU.mult, ALU.mult, t, t_b)
            tt("dve", x[:, p, :], x[:, p, :], qf[:, p, :], ALU.add, free[k])
        layer("L2a")

        (wq, wk, wv), tw = load_w(["L2q", "L2k", "L2v"])
        wo2 = big[0:8, 0:2048].rearrange("d (h n) -> d h n", h=H)
        P.dma(s_w, wo2, a["L2o"])
        bqv = big[0:8, 2048:2080].rearrange("d (k h) -> d k h", k=2)
        P.dma(s_w, bqv, a["L2b"])
        (bo2,), tw = rows_in(["L2bo"])
        n = layernorm(x, xn)
        transpose_all(xn, n, (xT, None, None))
        fold(64, 8, wq, wk, wv, wo2, True, tw)
        k, w = take()
        for h in range(H):
            for r in range(2):
                t = mm(bank(k)[64 * r:64 * r + 64, h:h + 1], wk[0:8, h, :], bqv[:, 0, h:h + 1], True, True, w, tw)
        qbias = small[:, 0:H]
        free[k] = cp("dve", qbias, bank(k, H), t)
        k, w = take()
        mm(bank(k, 128)[0:1], one[0:1, 0:1], bo2, True, False, w, sig=False)
        for h in range(H):
            t = mm(bank(k, 128)[0:1], bqv[:, 1, h:h + 1], wo2[:, h, :], False, h == H - 1)
        free[k] = cp("dve", crow[:, :], bank(k, 128)[0:1], t)
        layer("L2b")
        cross(8 ** -0.5, ctxN, ctxT, xT, x, bias=qbias)

        dft = wst[:, 0:384].rearrange("p (k n) -> p k n", k=3)
        P.dma(s_w, dft, a["dft"])
        wf = wst[:, 384:640].rearrange("p (k n) -> p k n", k=2)
        P.dma(s_w, wf, a["wfreq"])
        tw = P.dma(s_w, crow[:, :], a["L2bias"])
        n = layernorm(x, xn)
        t_x = transpose_all(xn, n, (xT, None, None))
        tq = wst[:, 640:896].rearrange("p (k n) -> p k n", k=2)
        mat = wst[:, 896:1024]
        cosm, sinm, nsin = dft[:, 0, :], dft[:, 1, :], dft[:, 2, :]
        k, w = take()
        mm(bank(k, 128), wf[:, 0, :], cosm, True, False, w, tw)
        mm(bank(k, 128), wf[:, 1, :], sinm, False, True)
        mm(bank(k)[:, 128:256], wf[:, 0, :], sinm, True, False)
        nw = ts(wst[:, 1024:1152], wf[:, 1, :], -1.0, None, ALU.mult, None, tw)
        t = mm(bank(k)[:, 128:256], wst[:, 1024:1152], cosm, False, True, nw)
        t = ts(tq, bank(k, 256).rearrange("p (k n) -> p k n", k=2), 1.0 / 128.0, None, ALU.mult, None, t)
        free[k] = t
        k, w = take()
        mm(bank(k, 128), tq[:, 0, :], cosm, True, False, w, t)
        t = mm(bank(k, 128), tq[:, 1, :], sinm, False, True)
        free[k] = t_m = cp("act", mat, bank(k, 128), t)
        for p in range(NP):
            k, w = take()
            mm(bank(k, 128), one[0:1, :], crow[:, :], True, False, w, tw, sig=False)
            t = mm(bank(k, 128), xT[:, 128 * p:128 * p + 128], mat, False, True, t_x, t_m)
            free[k] = tt("dve", x[:, p, :], x[:, p, :], bank(k, 128), ALU.add, t)
        layer("L3a")
        P.pending["sp"].append(stored)

        def load_v(name, tile):
            return P.dma(s_w, tile, a[name])

        vec = sb("vec", [128, 32])
        xn2 = sb("xn2", [128, NP, D])
        load_v("L3vec", vec[:, :])
        gb = cx[:, 2048:2816].rearrange("p (k n) -> p k n", k=6)
        tw = load_v("L3bc", gb)
        Lx = cx[:, 0:2048].rearrange("p (b d) -> p b d", b=NP)
        yb = xn
        yTt = cTs[:, 0:2048]

        def affine(buf, g, b, ready):
            g, b = (v.unsqueeze(1).broadcast_to([128, NP, D]) for v in (g, b))
            t = tt("dve", buf[:, :, :], buf[:, :, :], g, ALU.mult, sum(ready, []), tw)
            return [tt("dve", buf[:, :, :], buf[:, :, :], b, ALU.add, t)] * NP

        def mlp(src, dst, v0, l2, l3, brow, twm):
            n = layernorm(src, xn)
            t_x = transpose_all(xn, n, (xT, vec[:, v0:v0 + 1], vec[:, v0 + 1:v0 + 2]))
            hid = [big[:, 0:2048], big[:, 2048:4096]]
            zs = [zero("pool", h) for h in hid]
            use = [[], []]
            for c in range(4):
                u = c % 2
                hv = hid[u].rearrange("p (m n) -> p m n", m=4)
                t_h = []
                for m in range(4):
                    k, w = take()
                    t = mm(bank(k, 448), l2[:, m, :], tok8(xT, c), True, True, w, t_x, twm)
                    free[k] = act(hv[:, m, :].rearrange("p (b q) -> p b q", q=64)[:, :, 0:NQ], q8(k), ACT.Gelu,
                                  t, use[u], zs[u], bias=vec[:, v0 + 2 + m:v0 + 3 + m])
                    t_h += free[k]
                for q in range(4):
                    p = 4 * c + q
                    k, w = take()
                    mm(bank(k, 128), one[0:1, :], brow, True, False, w, sig=False)
                    for m in range(4):
                        t = mm(bank(k, 128), hv[:, m, 128 * q:128 * q + 128], l3[:, m, :], False, m == 3, t_h)
                    use[u] = t
                    free[k] = tt("dve", dst[:, p, :], dst[:, p, :], bank(k, 128), ALU.add, t)

        (wq, wk, wv), _ = load_w(["a1q", "a1k", "a1v"])
        woa = big[0:32, 0:2048].rearrange("d (h n) -> d h n", h=H)
        P.dma(s_w, woa, a["a1o"])
        (a1b1, a1b3, a2b1, a2b3), tw = rows_in(["a1b1", "a1b3", "a2b1", "a2b3"])
        for e in ("dve", "pool", "pe"):
            P.pending[e].append(tw)
        n = layernorm(x, xn)
        P.fence()
        n = layernorm(xn, Lx)
        n = affine(Lx, gb[:, 0, :], gb[:, 1, :], n)
        P.fence()
        n = layernorm(Lx, xn)
        t_x = transpose_all(xn, n, (xT, vec[:, 0:1], vec[:, 1:2]), (yTt, vec[:, 2:3], vec[:, 3:4]))
        fold(128, 32, wq, wk, wv, woa, False, tw)
        P.fence()
        for k in range(8):
            free[k] = []
        affine(yb, gb[:, 2, :], gb[:, 3, :], [[]] * NP)
        maskt = wst[:, 0:392].rearrange("p (j t) -> p j t", j=NJ)
        tw = P.dma(s_w, maskt, a["mask"])
        P.fence()
        P.pending["dve"].append(tw)

        Q1h, Q1l = Qh, Ql
        yh = cx[:, 2816:3840].bitcast(BF16)
        yl = cx[:, 3840:4864].bitcast(BF16)
        t = cp("act", yh, yTt)
        t_y = tt("dve", yl, yTt, yh, ALU.subtract, t)
        sE = [big[:, 14336 + 400 * i:14336 + 400 * i + 392].rearrange("p (j t) -> p j t", j=NJ) for i in range(2)]
        AT = [big[:, 15200 + 896 * i:15200 + 896 * i + 896] for i in range(2)]
        OTw = [big[:, 17024 + 2048 * i:17024 + 2048 * i + 2048] for i in range(2)]
        OTh, OTl = ([o[:, 1024 * n:1024 * n + 1024].bitcast(BF16).rearrange("c (h q) -> c h q", h=H) for o in OTw]
                    for n in range(2))
        zs = [zero("pool", o) for o in OTw]
        OT_use = [[], []]
        for b0 in range(0, B, HB):
            for c in range(HB // 8):
                for h in range(H):
                    k, w = take()
                    t = mm(bank(k, 448), wav[:, h, :], tok8(xT, b0 // 8 + c), True, True, w)
                    o = slice(8 * c, 8 * c + 8), slice(NQ * h, NQ * h + NQ)
                    t1 = act(Q1h[:, o[0], o[1]], q8(k), ACT.Copy, t)
                    t2 = tt("dve", Q1l[:, o[0], o[1]], q8(k), Q1h[:, o[0], o[1]], ALU.subtract, t, t1)
                    free[k] = t1 + t2
            P.fence()
            for k in range(8):
                free[k] = []
            sE_use, AT_use, t_a, t_ot = [[], []], [[], []], {}, {}
            o2_free, t2_free = [], []

            def soft(i):
                u = i % 2
                b = b0 + i
                v = small[:, 32 * u:32 * u + 28].rearrange("p (k j) -> p k j", k=4)
                keys = slice(64 * b, 64 * b + NQ)
                for j in range(NJ):
                    o = bank(u)[:, NQ * j:NQ * j + NQ]
                    cols = slice(128 * j, 128 * j + 128)
                    mm(o, Q1h[:, i, cols], yh[:, keys], True, False, free[u], t_y, sig=False)
                    mm(o, Q1h[:, i, cols], yl[:, keys], False, False, sig=False)
                    mm(o, Q1l[:, i, cols], yh[:, keys], False, False, sig=False)
                    t = mm(o, Q1l[:, i, cols], yl[:, keys], False, True, sig=(j == NJ - 1))
                pv = bank(u, 392).rearrange("p (j t) -> p j t", j=NJ)
                t1 = red(v[:, 0, :], pv, ALU.max, t)
                t1 = tt("dve", sE[u], pv, v[:, 0, :].unsqueeze(2).broadcast_to([128, NJ, NQ]), ALU.subtract, t1, sE_use[u])
                free[u] = t1
                t1 = act(sE[u], sE[u], ACT.Exp, t1, scale=32 ** -0.5)
                t2 = red(v[:, 1, :], sE[u], ALU.add, t1)
                t2 = put("dve", lambda g: g.reciprocal(v[:, 2, :], v[:, 1, :]), t2)
                t1 = tt("dve", sE[u], sE[u], maskt, ALU.mult, t1, t2)
                t_a[i] = tt("dve", sE[u], sE[u], v[:, 2, :].unsqueeze(2).broadcast_to([128, NJ, NQ]), ALU.mult, t1, t2)

            def apply(i):
                u, r = i % 2, i % 2
                pp = i // 2
                p = (b0 + i) // 2
                for j in range(NJ):
                    t = tr(ps[0:NQ, 1024 + 128 * j:1024 + 128 * j + 128], sE[u][:, j, :], idf[:, :], t2_free, t_a[i],
                           sig=(j == NJ - 1))
                sE_use[u] = t
                rows = slice(64 * r, 64 * r + NQ)
                t = cp("act", AT[u][rows, :], ps[0:NQ, 1024:1024 + HQ], t, AT_use[u])
                t2_free[:] = t
                for hf in range(2):
                    tm = mm(bank(4 + hf, 448), yb[rows, p, :], AT[u][rows, 448 * hf:448 * hf + 448], True, True,
                            t, o2_free, sig=(hf == 1))
                AT_use[u] = tm
                done = []
                for hf in range(2):
                    o = slice(8 * hf, 8 * hf + 8), slice(64 * r, 64 * r + NQ)
                    t1 = act(OTh[pp % 2][:, o[0], o[1]], q8(4 + hf), ACT.Copy, tm, OT_use[pp % 2], zs[pp % 2])
                    t2 = tt("dve", OTl[pp % 2][:, o[0], o[1]], q8(4 + hf), OTh[pp % 2][:, o[0], o[1]], ALU.subtract, t1,
                            OT_use[pp % 2], zs[pp % 2])
                    done += t1 + t2
                o2_free[:] = done
                t_ot[i] = done
                if r == 1:
                    k = 6 + pp % 2
                    mm(bank(k, 128), one[0:1, :], a1b1, True, False, free[k], sig=False)
                    for h in range(H):
                        mm(bank(k, 128), OTh[pp % 2][:, h, :], wbhv[:, h, :], False, False, t_ot[i], t_ot[i - 1], sig=False)
                        mm(bank(k, 128), OTh[pp % 2][:, h, :], wblv[:, h, :], False, False, sig=False)
                        mm(bank(k, 128), OTl[pp % 2][:, h, :], wbhv[:, h, :], False, False, sig=False)
                        t = mm(bank(k, 128), OTl[pp % 2][:, h, :], wblv[:, h, :], False, h == H - 1, sig=(h == H - 1))
                    OT_use[pp % 2] = t
                    free[k] = stt(xn2[:, p, :], Lx[:, p, :], 1.0, bank(k, 128), ALU.mult, ALU.add, t)

            soft(0)
            for i in range(HB):
                if i + 1 < HB:
                    soft(i + 1)
                apply(i)
            P.fence()
            for k in range(8):
                free[k] = []
        l2 = wst[:, 0:512].rearrange("p (m n) -> p m n", m=4)
        l3 = wst[:, 512:1024].rearrange("p (m n) -> p m n", m=4)
        P.dma(s_w, l2, a["a1l2"])
        tw = P.dma(s_w, l3, a["a1l3"])
        t = tt("dve", Lx[:, :, :], Lx[:, :, :], xn2[:, :, :], ALU.add)
        P.pending["dve"].append(t)
        mlp(xn2, Lx, 4, l2, l3, a1b3, tw)
        layer("L3f")

        (wq, wk, wv), tw = load_w(["a2q", "a2k", "a2v"])
        woa = big[0:32, 0:2048].rearrange("d (h n) -> d h n", h=H)
        tw = P.dma(s_w, woa, a["a2o"])
        n = layernorm(Lx, xn2)
        n = affine(xn2, gb[:, 4, :], gb[:, 5, :], n)
        P.fence()
        for p in range(NP):
            tt("pool", x[:, p, :], x[:, p, :], xn2[:, p, :], ALU.add)
        cp("act", crow[:, :], a2b1)
        n = layernorm(xn2, xn)
        transpose_all(xn, n, (xT, vec[:, 10:11], vec[:, 11:12]))
        fold(64, 32, wq, wk, wv, woa, True, tw)
        layer("L3h")
        cross(32 ** -0.5, yN, yT, xT, xn2)
        l2 = wst[:, 0:512].rearrange("p (m n) -> p m n", m=4)
        l3 = wst[:, 512:1024].rearrange("p (m n) -> p m n", m=4)
        P.dma(s_w, l2, a["a2l2"])
        tw = P.dma(s_w, l3, a["a2l3"])
        t = tt("dve", x[:, :, :], x[:, :, :], xn2[:, :, :], ALU.add)
        P.pending["dve"].append(t)
        mlp(xn2, x, 12, l2, l3, a2b3, tw)
        layer("L4")

        rw = wst[:, 0:16]
        P.dma(s_w, rw, a["routerT"])
        f1 = wst[:, 128:640].rearrange("p (m n) -> p m n", m=4)
        P.dma(s_w, f1, a["w1T"])
        f2 = wst[:, 640:1152].rearrange("p (m n) -> p m n", m=4)
        P.dma(s_w, f2, a["w2T"])
        tri = wst[:, 1152:1152 + 256].rearrange("p (i j) -> p i j", i=16)
        P.dma(s_w, tri, a["tri16"])
        spread = wst[0:16, 1408:1920].rearrange("p (m n) -> p m n", m=4)
        P.dma(s_w, spread, a["spread"])
        fb = wst[:, 1920:1924]
        P.dma(s_w, fb, a["f1b"])
        P.dma(s_w, crow[:, :], a["f2b"])
        rbr = rowb[0:1, 0:16]
        tw = P.dma(s_w, rbr, a["routerb"])
        n = layernorm(x, xn)
        t_x = transpose_all(xn, n, (xT, None, None))
        ve_big = big[:, 12288:12544]
        g1 = big[:, 0:4096].rearrange("p (b i j) -> p b i j", b=NP, i=16)
        g2 = big[:, 4096:8192].rearrange("p (b i j) -> p b i j", b=NP, i=16)
        lg = big[:, 12544:12800].rearrange("p (b e) -> p b e", b=NP)
        sel = big[:, 12800:13056].rearrange("p (b e) -> p b e", b=NP)
        selT = big[0:16, 13056:13056 + 2048]
        k, w = take()
        for p in range(NP):
            mm(bank(k)[:, 16 * p:16 * p + 16], xT[:, 128 * p:128 * p + 128], rw, True, False, w, tw, t_x, sig=False)
            t = mm(bank(k)[:, 16 * p:16 * p + 16], one[0:1, :], rbr, False, True)
        t = cp("dve", lg, bank(k, 256).rearrange("p (b e) -> p b e", b=NP), t)
        free[k] = t
        t = red(small[:, 0:NP], lg, ALU.max, t)
        t = tt("dve", lg, lg, small[:, 0:NP].unsqueeze(2).broadcast_to([128, NP, 16]), ALU.subtract, t)
        t = act(lg, lg, ACT.Exp, t)
        t = red(small[:, 16:16 + NP], lg, ALU.add, t)
        t = put("dve", lambda g: g.reciprocal(small[:, 32:32 + NP], small[:, 16:16 + NP]), t)
        t = tt("dve", lg, lg, small[:, 32:32 + NP].unsqueeze(2).broadcast_to([128, NP, 16]), ALU.mult, t)
        t_s = rank_sel(lg, NP, 16, 4, tri, sel, t, g1, g2)
        t_ct = []
        for g4 in range(4):
            k, w = take()
            for q in range(4):
                t = tr(bank(k)[0:16, 128 * q:128 * q + 128], sel[:, 4 * g4 + q, :], idf[:, :], w, t_s, sig=(q == 3))
            free[k] = cp("act", selT[:, 512 * g4:512 * g4 + 512], bank(k)[0:16, :], t)
            t_ct += free[k]
        hid = [big[:, 16384:18432], big[:, 18432:20480]]
        rel = [big[:, 8192 + 448 * i:8192 + 448 * i + 448] for i in range(4)]
        zs = [zero("pool", h) for h in hid]
        use, r_use = [[], []], [[] for _ in range(4)]
        for c in range(4):
            u = c % 2
            hv = hid[u].rearrange("p (m n) -> p m n", m=4)
            t_h = []
            for m in range(4):
                k1, w = take()
                t1 = mm(bank(k1, 448), f1[:, m, :], tok8(xT, c), True, True, w)
                k2, w = take()
                t2 = mm(bank(k2, 448), spread[:, m, :], tok8(selT, c), True, True, w, t_ct)
                free[k1] = act(rel[m], bank(k1, 448), ACT.Relu, t1, r_use[m], bias=fb[:, m:m + 1])
                free[k2] = tt("dve", hv[:, m, :].rearrange("p (b q) -> p b q", q=64)[:, :, 0:NQ], q8(k2),
                              rel[m].rearrange("p (b q) -> p b q", q=NQ), ALU.mult, t2, free[k1], use[u], zs[u])
                r_use[m] = free[k2]
                t_h += free[k2]
            for q in range(4):
                p = 4 * c + q
                k, w = take()
                mm(bank(k, 128), one[0:1, :], crow[:, :], True, False, w, sig=False)
                for m in range(4):
                    t = mm(bank(k, 128), hv[:, m, 128 * q:128 * q + 128], f2[:, m, :], False, m == 3, t_h)
                use[u] = t
                free[k] = tt("dve", x[:, p, :], x[:, p, :], bank(k, 128), ALU.add, t)
        ov = out.rearrange("(p r) q d -> r q p d", r=2)
        t = P.all_done()
        for r in range(2):
            t_out = P.dma(s_out, ov[r], x[64 * r:64 * r + NQ, :, :], t)
        ends = t_out + stored

        block = ctx.enter_context(nc.Block())

        @block.sync
        def _(eng):
            P.run("sp", eng)
            for s, v in ends:
                eng.wait_ge(s, v)

        @block.tensor
        def _(eng):
            P.run("pe", eng)

        @block.vector
        def _(eng):
            P.run("dve", eng)

        @block.scalar
        def _(eng):
            P.run("act", eng)

        @block.gpsimd
        def _(eng):
            P.run("pool", eng)


def layout(i):
    import numpy as np

    f = {}
    f["x"] = i["x"]
    c = i["ctx_512"].reshape(B, KP, KT, C)
    f["ctxN"] = c.reshape(B, KP, KT * C)
    f["ctxT"] = c.transpose(0, 3, 2, 1).reshape(B, C, M)
    g = np.arange(128)
    f["ident"] = np.eye(128, dtype=np.float32)

    def cols(w, d):
        return w.reshape(w.shape[0], H, d).transpose(2, 1, 0)

    def rows(w, d):
        return w.reshape(H, d, w.shape[1]).transpose(1, 0, 2)

    f["L0q"], f["L0k"], f["L0v"] = (cols(i[f"L0_xattn_W{n}"], 64) for n in "qkv")
    f["L0o"] = rows(i["L0_xattn_Wo"], 64)
    f["L0bo"] = i["L0_xattn_bo"].reshape(1, 128)
    f["Wgate"] = i["L0_ffn_Wgate"]
    f["bgate"] = i["L0_ffn_bgate"].reshape(1, E)
    w1, w2, w3 = (i[f"L0_ffn_W{n}"] for n in "123")

    def halves(w):
        return w.reshape(E, 2, 128, -1).transpose(0, 2, 1, 3).reshape(E, 128, -1)

    f["ew"] = np.concatenate([w1, w2, halves(i["L0_ffn_Wg"]), halves(i["L0_ffn_Wl"]),
                              np.zeros((E, 128, 512), np.float32)], axis=2)
    f["ew3"] = halves(w3)
    f["ebias"] = np.stack([i[f"L0_ffn_{n}"].reshape(E, 2, 128) for n in ("b1", "b2", "bg", "bl")], 1) \
        .transpose(3, 0, 1, 2).reshape(128, E, 8)
    f["b3"] = i["L0_ffn_b3"]
    for n in (8, 16):
        f[f"tri{n}"] = np.ascontiguousarray(np.broadcast_to(np.tril(np.ones((n, n), np.float32), -1), (128, n, n)))
    f["L1q"] = rows(i["L1_xattn_Wq"], 8)
    f["L1k"] = rows(i["L1_xattn_Wkv"][:128], 8)
    f["L1v"] = rows(i["L1_xattn_Wkv"][128:], 8)
    f["L1o"] = rows(i["L1_xattn_Wo"].T, 8)
    f["rhsT"] = i["L1_ffn_rhs"].T
    f["L2q"], f["L2k"], f["L2v"] = (cols(i[f"L2_xattn_W{n}"], 8) for n in "qkv")
    f["L2o"] = rows(i["L2_xattn_Wo"], 8)
    f["L2b"] = np.stack([i["L2_xattn_bq"].reshape(H, 8).T, i["L2_xattn_bv"].reshape(H, 8).T], 1)
    f["L2bo"] = i["L2_xattn_bo"].reshape(1, 128)
    ang = 2 * np.pi * (np.outer(g, g) % 128) / 128
    f["dft"] = np.stack([np.cos(ang), np.sin(ang), -np.sin(ang)], 1).astype(np.float32)
    f["wfreq"] = np.stack([i["L2_ffn_w_freq_real"], i["L2_ffn_w_freq_imag"]], 1)
    f["L2bias"] = i["L2_ffn_bias"].reshape(1, 128)
    for n in ("a1", "a2"):
        for w in "qkv":
            f[f"{n}{w}"] = i[f"L3_xattn_{n}_w{w}"].transpose(2, 0, 1)
        f[f"{n}o"] = rows(i[f"L3_xattn_{n}_li1_w"], 32)
        f[f"{n}b1"] = i[f"L3_xattn_{n}_li1_b"].reshape(1, 128)
        f[f"{n}b3"] = i[f"L3_xattn_{n}_li3_b"].reshape(1, 128)
        f[f"{n}l2"] = i[f"L3_xattn_{n}_li2_w"].reshape(128, 4, 128)
        f[f"{n}l3"] = i[f"L3_xattn_{n}_li3_w"].reshape(4, 128, 128).transpose(1, 0, 2)
    p = "L3_xattn_"

    def li2b(n):
        return list(i[f"{p}{n}_li2_b"].reshape(4, 128))

    zero = np.zeros(128, np.float32)
    v = [i[p + n] for n in ("a1_lnx_g", "a1_lnx_b", "a1_lny_g", "a1_lny_b", "a1_ln3_g", "a1_ln3_b")] + li2b("a1")
    v += [i[p + n] for n in ("a2_lnx_g", "a2_lnx_b", "a2_ln3_g", "a2_ln3_b")] + li2b("a2")
    f["L3vec"] = np.stack(v + [zero] * (32 - len(v)), 1)
    f["L3bc"] = np.ascontiguousarray(np.broadcast_to(np.stack(
        [i[p + n] for n in ("ln1_g", "ln1_b", "a1_lny_g", "a1_lny_b", "ln2_g", "ln2_b")]), (128, 6, 128)))
    f["a2lyg"], f["a2lyb"] = (np.ascontiguousarray(np.broadcast_to(i[p + n], (128, C))) for n in ("a2_lny_g", "a2_lny_b"))
    r = np.arange(HQ).reshape(NJ, 128).T % NQ
    f["mask"] = (np.arange(NQ)[None, None, :] > r[:, :, None]).astype(np.float32)
    f["routerT"] = i["L3_ffn_router_w"].T
    f["routerb"] = i["L3_ffn_router_b"].reshape(1, 16)
    f["w1T"] = i["L3_ffn_w1"].T.reshape(128, 4, 128)
    f["w2T"] = i["L3_ffn_w2"].T.reshape(4, 128, 128).transpose(1, 0, 2)
    f["f1b"] = i["L3_ffn_b1"].reshape(4, 128).T
    f["f2b"] = i["L3_ffn_b2"].reshape(1, 128)
    f["spread"] = (np.arange(16)[:, None] == np.arange(512)[None, :] // 32).astype(np.float32).reshape(16, 4, 128)
    return {n: np.ascontiguousarray(w) for n, w in f.items()}


def kernel(**inputs):
    import numpy as np
    import concourse.bacc as bacc
    from concourse import mybir as mb
    from concourse.bass_utils import run_bass_kernel_spmd

    nc = bacc.Bacc("TRN2", target_bir_lowering=False, num_devices=1)
    host = layout({n: np.asarray(v) for n, v in inputs.items()})
    arrays = {f"in_{n}": v for n, v in host.items()}
    aps = {n: nc.dram_tensor(f"in_{n}", v.shape, mb.dt.from_np(v.dtype), kind="ExternalInput").ap()
           for n, v in host.items()}
    out = nc.dram_tensor("out_x", (B, NQ, D), F32, kind="ExternalOutput").ap()
    build(nc, aps, out)
    r = run_bass_kernel_spmd(nc, [arrays], core_ids=[0])
    return r.results[0]["out_x"]
```
